# Optimizing a Trainium2 kernel written in Bass

```python
import numpy as np
import jax
import jax.numpy as jnp

def _softmax(x, axis=-1):
    return jax.nn.softmax(x, axis=axis)

def _gelu(x):
    return jax.nn.gelu(x, approximate=True)

def _silu(x):
    return jax.nn.silu(x)

def _sigmoid(x):
    return jax.nn.sigmoid(x)

def _layernorm(x, axis=-1, eps=1e-05):
    m = jnp.mean(x, axis=axis, keepdims=True)
    v = jnp.var(x, axis=axis, keepdims=True)
    return (x - m) / jnp.sqrt(v + eps)

def _scatter_add(tgt, idx, src, axis=0):
    return tgt.at[idx].add(src)

def _segment_sum(src, seg, n):
    return jax.ops.segment_sum(src, seg, n)
kernel_name = 'mk_audio_tower_d2_tok_audfeat256_r4_2e3963'

def setup_inputs(seed: int=0):
    np.random.seed(seed)
    _w = jnp.asarray

    def _rec_inputs():
        import jax
        import jax.numpy as jnp
        _rk = jax.random.key(seed)
        x = -5.07413e-05 + 0.999912 * jax.random.normal(jax.random.fold_in(_rk, 1), (128, 256, 64), jnp.float32)
        return x
    x = _rec_inputs()

    def _L0_tok_setup():
        import jax, jax.numpy as jnp
        from jax import lax
        import numpy as np
        B, T, C, K, STRIDE = (16, 4000, 64, 5, 2)
        EPS = 0.001
        key = jax.random.key(seed)
        k0, k1, k2, k3 = jax.random.split(key, 4)
        x = jax.random.normal(k0, (B, T, C), dtype=jnp.float32)
        w = jax.random.normal(k1, (K, 1, C), dtype=jnp.float32) * 0.1
        b = jax.random.normal(k2, (C,), dtype=jnp.float32) * 0.01
        gamma = jnp.ones((C,), dtype=jnp.float32)
        beta = jnp.zeros((C,), dtype=jnp.float32)
        alpha = jnp.full((C,), 0.25, dtype=jnp.float32) + 0.01 * jax.random.normal(k3, (C,), dtype=jnp.float32)
        return {'x': x, 'w': w, 'b': b, 'gamma': gamma, 'beta': beta, 'alpha': alpha}
    _L0_tok_all = _L0_tok_setup()
    _L0_tok_in = {k: v for k, v in _L0_tok_all.items() if k in ('w', 'b', 'gamma', 'beta', 'alpha')}
    del _L0_tok_all

    def _L0_attn_setup():
        import jax, jax.numpy as jnp
        import numpy as np
        B, N, DIM = (4, 1024, 64)
        key = jax.random.key(seed)
        k1, k2 = jax.random.split(key)
        x_e = jax.random.normal(k1, (B, N, DIM), dtype=jnp.float32)
        W = jax.random.normal(k2, (DIM, DIM), dtype=jnp.float32) * 0.05
        return {'x_e': x_e, 'W': W}
    _L0_attn_all = _L0_attn_setup()
    _L0_attn_in = {k: v for k, v in _L0_attn_all.items() if k in ('W',)}
    del _L0_attn_all

    def _L0_ffn_setup():
        import jax, jax.numpy as jnp
        import numpy as np
        DIM = 64
        HEADS = 8
        NUM_KEYS = 64
        NUM_KV = NUM_KEYS ** 2
        PK_TOPK = 16
        FINAL_TOPK = 16
        DIM_KEY = DIM // 2
        P = 2

        def _pk(x, Wq_pk, pk_keys):
            b, n, _ = x.shape
            q = (x @ Wq_pk).reshape(b, n, P, HEADS, DIM_KEY).transpose(2, 0, 1, 3, 4)
            sim = jnp.einsum('pbnhd,pkhd->pbnhk', q, pk_keys)
            scores, idx = jax.lax.top_k(sim, PK_TOPK)
            idx0 = idx[0]
            idx1 = idx[1] * NUM_KEYS
            index = (idx0[..., :, None] + idx1[..., None, :]).reshape(b, n, HEADS, PK_TOPK * PK_TOPK)
            score = (scores[0][..., :, None] + scores[1][..., None, :]).reshape(b, n, HEADS, PK_TOPK * PK_TOPK)
            final_scores, pk_idx = jax.lax.top_k(score, FINAL_TOPK)
            final_indices = jnp.take_along_axis(index, pk_idx, axis=-1)
            final_scores = jax.nn.softmax(final_scores, axis=-1)
            return (final_scores, final_indices)
        key = jax.random.key(seed)
        ks = jax.random.split(key, 7)
        b, n = (2, 256)
        std = 0.02
        x = jax.random.normal(ks[0], (b, n, DIM), dtype=jnp.float32)
        Wq_pk = jax.random.normal(ks[1], (DIM, P * HEADS * DIM_KEY), dtype=jnp.float32) * std
        pk_keys = jax.random.normal(ks[2], (P, NUM_KEYS, HEADS, DIM_KEY), dtype=jnp.float32) * std
        Wq = jax.random.normal(ks[3], (DIM, HEADS * DIM), dtype=jnp.float32) * std
        keys_table = jax.random.normal(ks[4], (NUM_KV * HEADS, DIM), dtype=jnp.float32) * std
        values_table = jax.random.normal(ks[5], (NUM_KV * HEADS, DIM), dtype=jnp.float32) * std
        Wo = jax.random.normal(ks[6], (DIM * HEADS, DIM), dtype=jnp.float32) * std
        return {'x': x, 'Wq_pk': Wq_pk, 'pk_keys': pk_keys, 'Wq': Wq, 'keys_table': keys_table, 'values_table': values_table, 'Wo': Wo}
    _L0_ffn_all = _L0_ffn_setup()
    _L0_ffn_in = {k: v for k, v in _L0_ffn_all.items() if k in ('Wq_pk', 'pk_keys', 'Wq', 'keys_table', 'values_table', 'Wo')}
    del _L0_ffn_all

    def _L1_attn_setup():
        import jax, jax.numpy as jnp
        import numpy as np
        HEADS = 8
        DIM = 64
        DIM_HEAD = 64
        DH = DIM_HEAD // HEADS
        SCALE = DIM_HEAD ** (-0.5)
        LN_EPS = 1e-05
        key = jax.random.key(seed)
        k1, k2, k3 = jax.random.split(key, 3)
        b, n = (8, 2048)
        x = jax.random.normal(k1, (b, n, DIM), dtype=jnp.float32)
        Wqkv = jax.random.normal(k2, (DIM, 3 * DIM_HEAD), dtype=jnp.float32) * 0.02
        Wout = jax.random.normal(k3, (DIM_HEAD, DIM), dtype=jnp.float32) * 0.02
        bout = jnp.zeros((DIM,), dtype=jnp.float32)
        gamma = jnp.ones((DIM,), dtype=jnp.float32)
        beta = jnp.zeros((DIM,), dtype=jnp.float32)
        return {'x': x, 'Wqkv': Wqkv, 'Wout': Wout, 'bout': bout, 'gamma': gamma, 'beta': beta}
    _L1_attn_all = _L1_attn_setup()
    _L1_attn_in = {k: v for k, v in _L1_attn_all.items() if k in ('Wqkv', 'Wout', 'bout', 'gamma', 'beta')}
    del _L1_attn_all

    def _L1_ffn_setup():
        import jax, jax.numpy as jnp
        import numpy as np
        E = 8
        K = 2
        D = 64
        H = 128
        DOUT = 64
        EPS = 1e-05
        key = jax.random.key(seed)
        ks = jax.random.split(key, 9)
        s = 0.02
        return {'x': jax.random.normal(ks[0], (4, 2048, D), jnp.float32), 'gamma': 1.0 + 0.05 * jax.random.normal(ks[1], (D,), jnp.float32), 'beta': 0.05 * jax.random.normal(ks[2], (D,), jnp.float32), 'Wr': 0.01 * jax.random.normal(ks[3], (D, E), jnp.float32), 'br': jnp.zeros((E,), jnp.float32), 'W1': s * jax.random.normal(ks[4], (E, D, H), jnp.float32), 'b1': s * jax.random.normal(ks[5], (E, H), jnp.float32), 'W2': s * jax.random.normal(ks[6], (E, H, DOUT), jnp.float32), 'b2': s * jax.random.normal(ks[7], (E, DOUT), jnp.float32)}
    _L1_ffn_all = _L1_ffn_setup()
    _L1_ffn_in = {k: v for k, v in _L1_ffn_all.items() if k in ('gamma', 'beta', 'Wr', 'br', 'W1', 'b1', 'W2', 'b2')}
    del _L1_ffn_all
    return {'x': x, 'L0_tok_w': _L0_tok_in['w'], 'L0_tok_b': _L0_tok_in['b'], 'L0_tok_gamma': _L0_tok_in['gamma'], 'L0_tok_beta': _L0_tok_in['beta'], 'L0_tok_alpha': _L0_tok_in['alpha'], 'L0_attn_W': _L0_attn_in['W'], 'L0_ffn_Wq_pk': _L0_ffn_in['Wq_pk'], 'L0_ffn_pk_keys': _L0_ffn_in['pk_keys'], 'L0_ffn_Wq': _L0_ffn_in['Wq'], 'L0_ffn_keys_table': _L0_ffn_in['keys_table'], 'L0_ffn_values_table': _L0_ffn_in['values_table'], 'L0_ffn_Wo': _L0_ffn_in['Wo'], 'L1_attn_Wqkv': _L1_attn_in['Wqkv'], 'L1_attn_Wout': _L1_attn_in['Wout'], 'L1_attn_bout': _L1_attn_in['bout'], 'L1_attn_gamma': _L1_attn_in['gamma'], 'L1_attn_beta': _L1_attn_in['beta'], 'L1_ffn_gamma': _L1_ffn_in['gamma'], 'L1_ffn_beta': _L1_ffn_in['beta'], 'L1_ffn_Wr': _L1_ffn_in['Wr'], 'L1_ffn_br': _L1_ffn_in['br'], 'L1_ffn_W1': _L1_ffn_in['W1'], 'L1_ffn_b1': _L1_ffn_in['b1'], 'L1_ffn_W2': _L1_ffn_in['W2'], 'L1_ffn_b2': _L1_ffn_in['b2']}

def reference(x, L0_tok_w, L0_tok_b, L0_tok_gamma, L0_tok_beta, L0_tok_alpha, L0_attn_W, L0_ffn_Wq_pk, L0_ffn_pk_keys, L0_ffn_Wq, L0_ffn_keys_table, L0_ffn_values_table, L0_ffn_Wo, L1_attn_Wqkv, L1_attn_Wout, L1_attn_bout, L1_attn_gamma, L1_attn_beta, L1_ffn_gamma, L1_ffn_beta, L1_ffn_Wr, L1_ffn_br, L1_ffn_W1, L1_ffn_b1, L1_ffn_W2, L1_ffn_b2):
    import jax
    import jax.numpy as jnp

    def _L0_tok_ref(x, w, b, gamma, beta, alpha):
        import jax, jax.numpy as jnp
        from jax import lax
        import numpy as np
        B, T, C, K, STRIDE = (16, 4000, 64, 5, 2)
        EPS = 0.001
        y = lax.conv_general_dilated(x, w, window_strides=(STRIDE,), padding='SAME', dimension_numbers=('NWC', 'WIO', 'NWC'), feature_group_count=C) + b
        mean = jnp.mean(y, axis=(1, 2), keepdims=True)
        var = jnp.var(y, axis=(1, 2), keepdims=True)
        yn = (y - mean) * lax.rsqrt(var + EPS) * gamma + beta
        return jnp.where(yn > 0, yn, alpha * yn)

    def _L0_attn_ref(x_e, W):
        import jax, jax.numpy as jnp
        import numpy as np
        B, N, DIM = (4, 1024, 64)
        W_masked = jnp.triu(W, k=1)
        x_e_ = jnp.einsum('bnt,st->bns', x_e, W_masked)
        logits = jnp.einsum('bnt,bmt->bnm', x_e_, x_e)
        out = jnp.einsum('bnm,bmt->bnt', logits, x_e)
        return out

    def _L0_ffn_ref(x, Wq_pk, pk_keys, Wq, keys_table, values_table, Wo):
        import jax, jax.numpy as jnp
        import numpy as np
        DIM = 64
        HEADS = 8
        NUM_KEYS = 64
        NUM_KV = NUM_KEYS ** 2
        PK_TOPK = 16
        FINAL_TOPK = 16
        DIM_KEY = DIM // 2
        P = 2

        def _pk(x, Wq_pk, pk_keys):
            b, n, _ = x.shape
            q = (x @ Wq_pk).reshape(b, n, P, HEADS, DIM_KEY).transpose(2, 0, 1, 3, 4)
            sim = jnp.einsum('pbnhd,pkhd->pbnhk', q, pk_keys)
            scores, idx = jax.lax.top_k(sim, PK_TOPK)
            idx0 = idx[0]
            idx1 = idx[1] * NUM_KEYS
            index = (idx0[..., :, None] + idx1[..., None, :]).reshape(b, n, HEADS, PK_TOPK * PK_TOPK)
            score = (scores[0][..., :, None] + scores[1][..., None, :]).reshape(b, n, HEADS, PK_TOPK * PK_TOPK)
            final_scores, pk_idx = jax.lax.top_k(score, FINAL_TOPK)
            final_indices = jnp.take_along_axis(index, pk_idx, axis=-1)
            final_scores = jax.nn.softmax(final_scores, axis=-1)
            return (final_scores, final_indices)
        b, n, d = x.shape
        q = (x @ Wq).reshape(b, n, HEADS, DIM) * DIM ** (-0.5)
        kv_scores, indices = _pk(x, Wq_pk, pk_keys)
        offsets = jnp.arange(HEADS, dtype=indices.dtype) * NUM_KV
        ind = indices + offsets[None, None, :, None]
        k = jnp.einsum('bnhk,bnhkd->bnhd', kv_scores, keys_table[ind])
        v = jnp.einsum('bnhk,bnhkd->bnhd', kv_scores, values_table[ind])
        sim = jnp.einsum('bihd,bjhd->bhij', q, k)
        neg = -jnp.finfo(sim.dtype).max
        causal = jnp.tril(jnp.ones((n, n), dtype=bool))
        sim = jnp.where(causal, sim, neg)
        attn = jax.nn.softmax(sim, axis=-1)
        out = jnp.einsum('bhij,bjhd->bhid', attn, v)
        out = out.transpose(0, 2, 1, 3).reshape(b, n, HEADS * DIM)
        return out @ Wo

    def _L1_attn_ref(x, Wqkv, Wout, bout, gamma, beta):
        import jax, jax.numpy as jnp
        import numpy as np
        HEADS = 8
        DIM = 64
        DIM_HEAD = 64
        DH = DIM_HEAD // HEADS
        SCALE = DIM_HEAD ** (-0.5)
        LN_EPS = 1e-05
        b, n, c = x.shape
        qkv = x @ Wqkv
        qkv = qkv.reshape(b, n, 3, HEADS, DH).transpose(2, 0, 3, 1, 4)
        q, k, v = (qkv[0], qkv[1], qkv[2])
        k = jax.nn.softmax(k, axis=-2)
        q = q * SCALE
        A = jnp.einsum('bhid,bhie->bhde', k, q)
        out = jnp.einsum('bhjd,bhde->bhje', v, A)
        out = out.reshape(b, n, c)
        out = out @ Wout + bout
        mu = jnp.mean(out, axis=-1, keepdims=True)
        var = jnp.var(out, axis=-1, keepdims=True)
        out = (out - mu) * jax.lax.rsqrt(var + LN_EPS) * gamma + beta
        return out

    def _L1_ffn_ref(x, gamma, beta, Wr, br, W1, b1, W2, b2):
        import jax, jax.numpy as jnp
        import numpy as np
        E = 8
        K = 2
        D = 64
        H = 128
        DOUT = 64
        EPS = 1e-05
        mu = jnp.mean(x, axis=-1, keepdims=True)
        var = jnp.mean(jnp.square(x - mu), axis=-1, keepdims=True)
        xn = (x - mu) * jax.lax.rsqrt(var + EPS) * gamma + beta
        logits = jnp.einsum('bsd,de->bse', xn, Wr) + br
        top_vals, top_idx = jax.lax.top_k(logits, K)
        w = jax.nn.softmax(top_vals, axis=-1)
        w_full = jnp.einsum('bsk,bske->bse', w, jax.nn.one_hot(top_idx, E, dtype=w.dtype))
        y = jnp.zeros(x.shape[:-1] + (DOUT,), x.dtype)
        for e in range(E):
            h = jax.nn.gelu(jnp.einsum('bsd,dh->bsh', xn, W1[e]) + b1[e], approximate=False)
            y_e = jnp.einsum('bsh,hd->bsd', h, W2[e]) + b2[e]
            y = y + y_e * w_full[..., e, None]
        return y
    h = _L0_tok_ref(x, L0_tok_w, L0_tok_b, L0_tok_gamma, L0_tok_beta, L0_tok_alpha)
    h = h + _L0_attn_ref(_layernorm(h, axis=-1), L0_attn_W)
    h = h + _L0_ffn_ref(_layernorm(h, axis=-1), L0_ffn_Wq_pk, L0_ffn_pk_keys, L0_ffn_Wq, L0_ffn_keys_table, L0_ffn_values_table, L0_ffn_Wo)
    h = h + _L1_attn_ref(_layernorm(h, axis=-1), L1_attn_Wqkv, L1_attn_Wout, L1_attn_bout, L1_attn_gamma, L1_attn_beta)
    h = h + _L1_ffn_ref(_layernorm(h, axis=-1), L1_ffn_gamma, L1_ffn_beta, L1_ffn_Wr, L1_ffn_br, L1_ffn_W1, L1_ffn_b1, L1_ffn_W2, L1_ffn_b2)
    return h

_drawn_inputs = setup_inputs


def setup_inputs(seed=0):
    import zlib

    import numpy as np

    out = dict(_drawn_inputs(seed))
    spreads = {'L0_tok_gamma': (1.0, 0.2),
     'L0_tok_beta': (0.0, 0.1),
     'L1_attn_bout': (0.0, 2.0),
     'L1_attn_gamma': (1.0, 0.6),
     'L1_attn_beta': (0.0, 2.0),
     'L1_ffn_br': (0.0, 0.8)}
    factors = {'L0_ffn_Wq_pk': 64.0,
     'L0_ffn_pk_keys': 64.0,
     'L0_ffn_Wq': 64.0,
     'L0_ffn_keys_table': 64.0,
     'L0_ffn_values_table': 64.0,
     'L0_ffn_Wo': 64.0,
     'L1_attn_Wqkv': 24.092,
     'L1_attn_Wout': 23.963,
     'L1_ffn_gamma': 8.0,
     'L1_ffn_beta': 22.703,
     'L1_ffn_Wr': 8.0,
     'L1_ffn_W1': 8.0,
     'L1_ffn_b1': 64.0,
     'L1_ffn_W2': 8.0,
     'L1_ffn_b2': 200.0}
    for name, (base, spread) in spreads.items():
        noise = np.random.default_rng([zlib.crc32(name.encode()), seed]).standard_normal(out[name].shape)
        drawn = base * np.exp(spread * noise) if base else spread * noise
        out[name] = jnp.asarray(drawn.astype(out[name].dtype))
    for name, factor in factors.items():
        out[name] = (out[name] * factor).astype(out[name].dtype)
    return out
```

```python
from contextlib import ExitStack

import concourse.bass as bass
from concourse import mybir

F32 = mybir.dt.float32
U32 = mybir.dt.uint32
I32 = mybir.dt.int32
ALU = mybir.AluOpType
ACT = mybir.ActivationFunctionType
AX = mybir.AxisListType

B, T_IN, C = 128, 256, 64
TAPS, STRIDE = 5, 2
T = T_IN // STRIDE
PAD_LOW = ((T - 1) * STRIDE + TAPS - T_IN) // 2
HEADS, SIDES, SUBKEYS, DKEY = 8, 2, 64, 32
GROUPS = SIDES * HEADS
TOPK = 16
KV = 2 * C
E, HID = 8, 128
L1_HEADS = 8
NEG = -3.0e38
EPS_TOK, EPS = 1e-3, 1e-5
Q_SCALE = C ** -0.5

SEGMENTS = []
_off = 0
for _r0, _rows in ((0, 1), (1, 1), (2, 1), (3, 1), (4, 1), (5, 3), (8, 8)):
    _w = TOPK // (_r0 + 1)
    SEGMENTS.append((_r0, _rows, _w, _off))
    _off += _rows * _w
CAND = _off

ROWS = {}
_at = 0
for _name, _n in (("conv_w", TAPS * C), ("conv_b", C), ("tok_gamma", C), ("tok_beta", C), ("tok_alpha", C),
                  ("bout", C), ("l1_gamma", C), ("l1_beta", C), ("ffn_gamma", C), ("ffn_beta", C),
                  ("br", E), ("b2", E * C)):
    ROWS[_name] = (_at, _at + _n)
    _at += _n
ROW_WORDS = _at
N_CONST_DMAS = 12


def build(nc, x, rows, w_mask_src, wqpk_t, keys_t, wq, table, wo, wqkv, wout, wr, w1, b1_t, w2, out):
    ctx = ExitStack()

    def sb(name, shape, dt=F32):
        return ctx.enter_context(nc.sbuf_tensor(name, shape, dt))

    def sem(name):
        return ctx.enter_context(nc.semaphore(name))

    def psum(name, shape):
        return ctx.enter_context(nc.psum_tensor(name, shape, F32))

    row = sb("row_consts", [T, ROW_WORDS])
    ident = sb("ident", [128, 128])
    mean_w = sb("mean_w", [128, 128])
    causal = sb("causal", [T, T])
    block8 = sb("block8", [C, C])
    iota_cand = sb("iota_cand", [T, CAND])
    iota_e = sb("iota_e", [T, E])
    table_base = sb("table_base", [T, HEADS])
    attn_w = sb("attn_w", [C, C])
    score_w = sb("score_w", [C, GROUPS * SUBKEYS])
    wq_sb = sb("wq_sb", [C, HEADS * C])
    wo_sb = sb("wo_sb", [128, HEADS * C // 128, C])
    wqkv_sb = sb("wqkv_sb", [C, 3 * C])
    wout_sb = sb("wout_sb", [C, L1_HEADS, C])
    wr_sb = sb("wr_sb", [C, E])
    w1_sb = sb("w1_sb", [C, E, HID])
    b1_sb = sb("b1_sb", [HID, E])
    w2_sb = sb("w2_sb", [HID, E, C])

    def rc(name):
        a, b = ROWS[name]
        return row[:, a:b]

    xwin = [sb(f"xwin{p}", [T, TAPS, C]) for p in range(2)]
    taps = sb("taps", [T, TAPS, C])
    y = sb("y", [T, C])
    stats6 = sb("stats6", [T, 6])
    rowstat = sb("rowstat", [T, 2])
    dev = sb("dev", [T, 1])
    dev_sq = sb("dev_sq", [T, 1])
    tok_mean = sb("tok_mean", [T, 1])
    f_var = sb("f_var", [T, 1])
    f_rstd0 = sb("f_rstd0", [T, 1])
    f_log = sb("f_log", [T, 1])
    f_tmp = sb("f_tmp", [T, 2])
    f_rstd = sb("f_rstd", [T, 1])
    yn, neg_part = taps[:, 0, :], taps[:, 1, :]
    h0 = sb("h0", [T, C])
    xh1 = sb("xh1", [T, C])
    xh1_t = sb("xh1_t", [C, T])
    gram = sb("gram", [C, C])
    attn_m = sb("attn_m", [C, C])
    h1 = [sb(f"h1_{p}", [T, C]) for p in range(2)]
    xh2 = sb("xh2", [T, C])
    xh2_t = [sb(f"xh2_t{p}", [C, T]) for p in range(2)]
    top = sb("top", [T, SIDES, HEADS, TOPK])
    top_i = sb("top_i", [T, SIDES, HEADS, TOPK], U32)
    top_f = sb("top_f", [T, SIDES, HEADS, TOPK])
    sim_rest = sb("sim_rest", [T, GROUPS, SUBKEYS])
    cand = sb("cand", [T, HEADS, CAND])
    cand_rest = sb("cand_rest", [T, HEADS, CAND])
    cand_i = sb("cand_i", [T, HEADS, CAND])
    fin = sb("fin", [T, HEADS, TOPK])
    pos_i = sb("pos_i", [T, HEADS, TOPK], U32)
    pos_f = sb("pos_f", [T, HEADS, TOPK])
    HH = HEADS // 4
    onehot = sb("onehot", [T, HH, TOPK, CAND])
    idx_f = sb("idx_f", [T, HEADS, TOPK])
    idx = [sb(f"idx{p}", [T, HEADS * TOPK], I32) for p in range(2)]
    fin_d = sb("fin_d", [T, HEADS, TOPK])
    fin_e = sb("fin_e", [T, HEADS, TOPK])
    fin_s = sb("fin_s", [T, HEADS])
    fin_r = sb("fin_r", [T, HEADS])
    kv_w = [sb(f"kv_w{p}", [T, HEADS, TOPK]) for p in range(2)]
    gath = [sb(f"gath{p}", [T, HEADS, TOPK, KV]) for p in range(2)]
    wqpk_sb = gath[1][0:DKEY, 0, 0:8, :].rearrange("d k c -> d (k c)").rearrange("d (g c) -> d g c", g=GROUPS)
    keys_sb = gath[1][0:DKEY, 1, 0:8, :].rearrange("d k c -> d (k c)").rearrange("d (g c) -> d g c", g=GROUPS)
    q_t = sb("q_t", [C, HEADS, T])
    kv = sb("kv", [T, HEADS, KV])
    k_t = sb("k_t", [C, HEADS, T])
    prob = sb("prob", [T, HEADS, T])
    neg_max = sb("neg_max", [T, HEADS])
    row_sum = sb("row_sum", [T, HEADS])
    row_inv = sb("row_inv", [T, HEADS])
    prob_t = sim_rest[:, :, :].rearrange("t g k -> t (g k)").rearrange("t (h i) -> t h i", h=HEADS)
    attn_o = sb("attn_o", [T, HEADS * C])
    attn_o_t = sb("attn_o_t", [128, HEADS * C // 128, T])
    b_stats6 = sb("b_stats6", [T, 6])
    b_mv = sb("b_mv", [T, 2])
    b_var = sb("b_var", [T, 1])
    b_rstd0 = sb("b_rstd0", [T, 1])
    b_log = sb("b_log", [T, 1])
    b_tmp = sb("b_tmp", [T, 2])
    b_rstd = sb("b_rstd", [T, 1])
    h2 = sb("h2", [T, C])
    xh3 = sb("xh3", [T, C])
    xh3_t = sb("xh3_t", [C, T])
    l1_q = sb("l1_q", [T, C])
    l1_v_t = sb("l1_v_t", [C, T])
    neg_kmax = sb("neg_kmax", [C, 1])
    ek_t = sb("ek_t", [C, T])
    k_sum = sb("k_sum", [C, 1])
    k_inv = sb("k_inv", [C, 1])
    ek = sb("ek", [T, C])
    l1_a = sb("l1_a", [C, C])
    l1_x = k_t[:, :, :].rearrange("d h t -> d (h t)").rearrange("d (j h m) -> d j h m", j=L1_HEADS, h=L1_HEADS)
    z = sb("z", [T, C])
    h3 = sb("h3", [T, C])
    xn = sb("xn", [T, C])
    xn_t = sb("xn_t", [C, T])
    logit = sb("logit", [T, E])
    best = sb("best", [T, 8])
    best_i = sb("best_i", [T, 8], U32)
    best_f = sb("best_f", [T, 2])
    gap = sb("gap", [T, 1])
    gap_e = sb("gap_e", [T, 1])
    gap_d = sb("gap_d", [T, 1])
    mix = sb("mix", [T, 2])
    pick = sb("pick", [T, 2, E])
    w_full = sb("w_full", [T, E])
    hid = prob
    y_e = attn_o[:, :].rearrange("t (e c) -> t e c", e=E)
    y_sum = sb("y_sum", [T, C])
    h_out = [sb(f"h_out{p}", [T, C]) for p in range(2)]

    p_front = psum("p_front", [128, 512])
    p_sim = psum("p_sim", [128, 1024])
    p_back = psum("p_back", [128, 512])
    p_x = psum("p_x", [128, 1024])
    p_y = psum("p_y", [128, 1024])

    consts_loaded = sem("consts_loaded")
    pool_consts = sem("pool_consts")
    pool_ones = sem("pool_ones")
    score_mm = sem("score_mm")
    score_ready = sem("score_ready")
    x_loaded = [sem(f"x_loaded{p}") for p in range(2)]
    conv_done = sem("conv_done")
    f_var_ready = sem("f_var_ready")
    f_rstd_ready = sem("f_rstd_ready")
    rowstats_ready = sem("rowstats_ready")
    mean_ready = sem("mean_ready")
    dev_ready = sem("dev_ready")
    var_ready = sem("var_ready")
    xh1_ready = sem("xh1_ready")
    gram_mm = sem("gram_mm")
    gram_ready = sem("gram_ready")
    attn_m_mm = sem("attn_m_mm")
    attn_m_ready = sem("attn_m_ready")
    attn0_mm = sem("attn0_mm")
    xh2_ready = sem("xh2_ready")
    xh2_tr = sem("xh2_tr")
    xh2_t_ready = sem("xh2_t_ready")
    sim_mm = sem("sim_mm")
    idx_ready = sem("idx_ready")
    fin_d_ready = sem("fin_d_ready")
    fin_e_ready = sem("fin_e_ready")
    kv_w_ready = sem("kv_w_ready")
    gathered = [[sem(f"gathered{p}_{h}") for h in range(HEADS)] for p in range(2)]
    scaled = sem("scaled")
    kv_mm = sem("kv_mm")
    kv_ready = sem("kv_ready")
    q_mm = sem("q_mm")
    q_ready = sem("q_ready")
    k_tr = sem("k_tr")
    k_t_ready = sem("k_t_ready")
    s_mm = sem("s_mm")
    neg_max_ready = sem("neg_max_ready")
    prob_ready = sem("prob_ready")
    prob_tr = sem("prob_tr")
    prob_t_ready = sem("prob_t_ready")
    attn_mm = sem("attn_mm")
    attn_o_ready = sem("attn_o_ready")
    attn_o_tr = sem("attn_o_tr")
    attn_o_t_ready = sem("attn_o_t_ready")
    wo_mm = sem("wo_mm")
    b_var_ready = sem("b_var_ready")
    b_rstd_ready = sem("b_rstd_ready")
    xh3_ready = sem("xh3_ready")
    xh3_tr = sem("xh3_tr")
    xh3_t_ready = sem("xh3_t_ready")
    qkv_mm = sem("qkv_mm")
    neg_kmax_ready = sem("neg_kmax_ready")
    ek_t_ready = sem("ek_t_ready")
    ek_tr = sem("ek_tr")
    ek_ready = sem("ek_ready")
    l1_a_mm = sem("l1_a_mm")
    l1_a_ready = sem("l1_a_ready")
    l1_o_mm = sem("l1_o_mm")
    l1_x_ready = sem("l1_x_ready")
    l1_mm = sem("l1_mm")
    xn_ready = sem("xn_ready")
    xn_tr = sem("xn_tr")
    xn_t_ready = sem("xn_t_ready")
    logit_mm = sem("logit_mm")
    gap_ready = sem("gap_ready")
    gap_e_ready = sem("gap_e_ready")
    hid_mm = sem("hid_mm")
    hid_ready = sem("hid_ready")
    y_mm = sem("y_mm")
    out_ready = sem("out_ready")
    out_free = [sem(f"out_free{p}") for p in range(2)]

    waits_passed = sem("waits_passed")

    BUILT = 6

    def hold(eng, s, value):
        eng.wait_ge(s, value)
        eng.sem_inc(waits_passed, 1)

    def over_batches(eng, front, back):
        front(0, 0)
        with eng.Fori(0, B // 2 - 1) as it:
            for p in range(2):
                front(it + (p + 1) // 2, 1 - p)
                back(it, p)
        front(B // 2 - 1, 1)
        back(B // 2 - 1, 0)
        back(B // 2 - 1, 1)

    block = ctx.enter_context(nc.Block())

    @block.sync
    def _(sp):
        for dst, src in ((row[:, :], rows), (attn_w[:, :], w_mask_src), (wqpk_sb[:, :, :], wqpk_t),
                         (keys_sb[:, :, :], keys_t), (wq_sb[:, :], wq), (wo_sb[:, :, :], wo),
                         (wqkv_sb[:, :], wqkv), (wout_sb[:, :, :], wout), (wr_sb[:, :], wr)):
            sp.dma_start(dst, src).then_inc(consts_loaded, 16)

        def load_window(it, p):
            b = 2 * it + p
            xb = x[b] if isinstance(b, int) else x[bass.ds(b, 1)].rearrange("o t c -> (o t) c")
            w = xwin[p]
            sp.dma_start(w[:, 1:3, :], xb.rearrange("(t k) c -> t k c", k=2)).then_inc(x_loaded[p], 16)
            sp.dma_start(w[1:T, 0, :], xb.rearrange("(t k) c -> t k c", k=2)[0:T - 1, 1, :]
                         ).then_inc(x_loaded[p], 16)
            sp.dma_start(w[0:T - 1, 3:5, :], xb.rearrange("(t k) c -> t k c", k=2)[1:T, :, :]
                         ).then_inc(x_loaded[p], 16)

        def store(it, p):
            b = 2 * it + p
            ob = out[b] if isinstance(b, int) else out[bass.ds(b, 1)].rearrange("o t c -> (o t) c")
            sp.wait_ge(out_ready, b + 1)
            sp.dma_start(ob, h_out[p][:, :]).then_inc(out_free[p], 16)

        sp.sem_inc(out_free[0], 16)
        sp.sem_inc(out_free[1], 16)
        sp.wait_ge(pool_ones, BUILT)
        load_window(0, 0)
        load_window(0, 1)
        sp.wait_ge(conv_done, 1)
        load_window(1, 0)
        with sp.Fori(0, B // 2 - 2) as it:
            for p in range(2):
                sp.wait_ge(conv_done, 2 * it + p + 2)
                load_window(it + 1 + p, 1 - p)
                store(it, p)
        sp.wait_ge(conv_done, B - 2)
        load_window(B // 2 - 1, 1)
        store(B // 2 - 2, 0)
        store(B // 2 - 2, 1)
        store(B // 2 - 1, 0)
        store(B // 2 - 1, 1)
        for p in range(2):
            sp.wait_ge(out_free[p], 16 * (B // 2 + 1))

    @block.gpsimd
    def _(pool):
        nc.gpsimd.memset(ident[:, :], 0.0).then_inc(pool_ones, 1)
        nc.gpsimd.memset(causal[:, :], 0.0).then_inc(pool_ones, 1)
        nc.gpsimd.memset(block8[:, :], 1.0).then_inc(pool_ones, 1)
        nc.gpsimd.memset(mean_w[:, :], 1.0 / 128).then_inc(pool_ones, 1)
        for p in range(2):
            nc.gpsimd.memset(xwin[p][:, :, :].rearrange("t k c -> t (k c)"), 0.0).then_inc(pool_ones, 1)
        pool.wait_ge(pool_ones, BUILT)
        nc.gpsimd.affine_select(out=ident[:, :], in_=ident[:, :], pattern=[[-1, 128]], compare_op=ALU.not_equal,
                                fill=1.0, base=0, channel_multiplier=1).then_inc(pool_consts, 1)
        nc.gpsimd.affine_select(out=causal[:, :], in_=causal[:, :], pattern=[[-1, T]], compare_op=ALU.is_ge,
                                fill=NEG, base=0, channel_multiplier=1).then_inc(pool_consts, 1)
        b8 = block8[:, :].rearrange("r (g j) -> r g j", g=L1_HEADS)
        nc.gpsimd.affine_select(out=b8, in_=b8, pattern=[[-8, L1_HEADS], [0, 8]], compare_op=ALU.is_ge,
                                fill=0.0, base=0, channel_multiplier=1).then_inc(pool_consts, 1)
        pool.wait_ge(pool_consts, 3)
        nc.gpsimd.affine_select(out=b8, in_=b8, pattern=[[8, L1_HEADS], [0, 8]], compare_op=ALU.is_ge,
                                fill=0.0, base=7, channel_multiplier=-1).then_inc(pool_consts, 1)
        nc.gpsimd.iota(iota_cand[:, :], pattern=[[1, CAND]], base=0, channel_multiplier=0,
                       allow_small_or_imprecise_dtypes=True).then_inc(pool_consts, 1)
        nc.gpsimd.iota(iota_e[:, :], pattern=[[1, E]], base=0, channel_multiplier=0,
                       allow_small_or_imprecise_dtypes=True).then_inc(pool_consts, 1)
        nc.gpsimd.iota(table_base[:, :], pattern=[[SUBKEYS * SUBKEYS, HEADS]], base=0, channel_multiplier=0,
                       allow_small_or_imprecise_dtypes=True).then_inc(pool_consts, 1)
        pool.wait_ge(consts_loaded, 16 * N_CONST_DMAS)
        nc.gpsimd.affine_select(out=attn_w[:, :], in_=attn_w[:, :], pattern=[[1, C]], compare_op=ALU.is_gt,
                                fill=0.0, base=0, channel_multiplier=-1).then_inc(pool_consts, 1)

        def front(it, p):
            pass

        def back(it, p):
            hold(pool, idx_ready, 2 * it + p + 1)
            for h in range(HEADS):
                for k in range(TOPK):
                    c = h * TOPK + k
                    nc.gpsimd.indirect_dma_start(
                        out=gath[p][:, h, k, :], out_offset=None, in_=table[:, :],
                        in_offset=bass.IndirectOffsetOnAxis(ap=idx[p][:, c:c + 1], axis=0),
                    ).then_inc(gathered[p][h], 16)

        over_batches(pool, front, back)

    @block.vector
    def _(dve):
        V = nc.vector
        V_sync = dve.drain

        def normalise(dst, src, mean, rstd):
            V.tensor_scalar(dst, src, mean, rstd, ALU.subtract, ALU.mult)

        def newton(var, r0, tmp, dst):
            V.scalar_tensor_tensor(tmp[:, 0:1], r0[:, :], r0[:, 0:1], var[:, :], ALU.mult, ALU.mult)
            V_sync()
            V.tensor_scalar(tmp[:, 1:2], tmp[:, 0:1], -0.5, 1.5, ALU.mult, ALU.add)
            V_sync()
            V.tensor_tensor(dst[:, :], r0[:, :], tmp[:, 1:2], ALU.mult)
            V_sync()

        def front_stats(src, nth, b):
            V.bn_stats(stats6[:, :], src)
            V_sync()
            V.bn_aggr(rowstat[:, :], stats6[:, :])
            V_sync()
            V.tensor_scalar(f_var[:, :], rowstat[:, 1:2], EPS, None, ALU.add).then_inc(f_var_ready, 1)
            dve.wait_ge(f_rstd_ready, 3 * b + nth)
            newton(f_var, f_rstd0, f_tmp, f_rstd)

        def back_stats(src, nth, b):
            V.bn_stats(b_stats6[:, :], src)
            V_sync()
            V.bn_aggr(b_mv[:, :], b_stats6[:, :])
            V_sync()
            V.tensor_scalar(b_var[:, :], b_mv[:, 1:2], EPS, None, ALU.add).then_inc(b_var_ready, 1)
            dve.wait_ge(b_rstd_ready, 4 * b + nth)
            newton(b_var, b_rstd0, b_tmp, b_rstd)

        def tokenizer(it, p):
            b = 2 * it + p
            dve.wait_ge(x_loaded[p], 48 * it + 48)
            V.tensor_tensor(taps[:, :, :], xwin[p][:, :, :],
                            rc("conv_w").rearrange("t (k c) -> t k c", k=TAPS), ALU.mult).then_inc(conv_done, 1)
            V_sync()
            V.tensor_reduce(y[:, :], taps[:, :, :].rearrange("t k c -> t c k"), AX.X, ALU.add)
            V_sync()
            V.tensor_tensor(y[:, :], y[:, :], rc("conv_b"), ALU.add)
            V_sync()
            V.bn_stats(stats6[:, :], y[:, :])
            V_sync()
            V.bn_aggr(rowstat[:, :], stats6[:, :]).then_inc(rowstats_ready, 1)
            V_sync()
            dve.wait_ge(mean_ready, b + 1)
            V.tensor_copy(tok_mean[:, :], p_front[:, 0:1])
            V_sync()
            V.tensor_tensor(dev[:, :], rowstat[:, 0:1], tok_mean[:, :], ALU.subtract)
            V_sync()
            V.scalar_tensor_tensor(dev_sq[:, :], dev[:, :], dev[:, 0:1], rowstat[:, 1:2], ALU.mult,
                                   ALU.add).then_inc(dev_ready, 1)
            dve.wait_ge(var_ready, b + 1)
            V.tensor_scalar(f_var[:, :], p_front[:, 1:2], EPS_TOK, None, ALU.add).then_inc(f_var_ready, 1)
            dve.wait_ge(f_rstd_ready, 3 * b + 1)
            newton(f_var, f_rstd0, f_tmp, f_rstd)
            normalise(yn, y[:, :], tok_mean[:, 0:1], f_rstd[:, 0:1])
            V_sync()
            V.tensor_tensor(yn, yn, rc("tok_gamma"), ALU.mult)
            V_sync()
            V.tensor_tensor(yn, yn, rc("tok_beta"), ALU.add)
            V_sync()
            V.scalar_tensor_tensor(neg_part, yn, 0.0, rc("tok_alpha"), ALU.min, ALU.mult)
            V_sync()
            V.scalar_tensor_tensor(h0[:, :], yn, 0.0, neg_part, ALU.max, ALU.add)
            V_sync()
            front_stats(h0[:, :], 2, b)
            normalise(xh1[:, :], h0[:, :], rowstat[:, 0:1], f_rstd[:, 0:1])
            V_sync()
            dve.sem_inc(xh1_ready, 1)

        def select(it, p):
            b = 2 * it + p
            dve.wait_ge(attn0_mm, b + 1)
            V.tensor_tensor(h1[p][:, :], h0[:, :], p_front[:, 384:448], ALU.add)
            V_sync()
            front_stats(h1[p][:, :], 3, b)
            normalise(xh2[:, :], h1[p][:, :], rowstat[:, 0:1], f_rstd[:, 0:1])
            V_sync()
            dve.sem_inc(xh2_ready, 1)
            hold(dve, sim_mm, b + 1)
            sim = p_sim[:, :].rearrange("t (g k) -> t g k", g=GROUPS)
            tops = top[:, :, :, :].rearrange("t s h k -> t (s h) k")
            tops_i = top_i[:, :, :, :].rearrange("t s h k -> t (s h) k")
            for g in range(GROUPS):
                V.max(tops[:, g, 0:8], sim[:, g, :])
            V_sync()
            for g in range(GROUPS):
                V.max_index(tops_i[:, g, 0:8], tops[:, g, 0:8], sim[:, g, :])
                V.match_replace(sim_rest[:, g, :], tops[:, g, 0:8], sim[:, g, :], NEG)
            V_sync()
            for g in range(GROUPS):
                V.max(tops[:, g, 8:16], sim_rest[:, g, :])
            V_sync()
            for g in range(GROUPS):
                V.max_index(tops_i[:, g, 8:16], tops[:, g, 8:16], sim_rest[:, g, :])
            V_sync()
            V.tensor_tensor(top_f[:, 0], top_i[:, 0], table_base[:, :, None].to_broadcast([T, HEADS, TOPK]),
                            ALU.add)
            V.tensor_scalar(top_f[:, 1], top_i[:, 1], float(SUBKEYS), None, ALU.mult)
            V_sync()
            for src, dst in ((top, cand), (top_f, cand_i)):
                for r0, n, w, off in SEGMENTS:
                    o = dst[:, :, off:off + n * w].rearrange("t h (r c) -> t h r c", r=n)
                    a = src[:, 0, :, r0:r0 + n, None].to_broadcast([T, HEADS, n, w])
                    c = src[:, 1, :, None, 0:w].to_broadcast([T, HEADS, n, w])
                    V.tensor_tensor(o, a, c, ALU.add)
            V_sync()
            for h in range(HEADS):
                V.max(fin[:, h, 0:8], cand[:, h, :])
            V_sync()
            for h in range(HEADS):
                V.max_index(pos_i[:, h, 0:8], fin[:, h, 0:8], cand[:, h, :])
                V.match_replace(cand_rest[:, h, :], fin[:, h, 0:8], cand[:, h, :], NEG)
            V_sync()
            for h in range(HEADS):
                V.max(fin[:, h, 8:16], cand_rest[:, h, :])
            V_sync()
            for h in range(HEADS):
                V.max_index(pos_i[:, h, 8:16], fin[:, h, 8:16], cand_rest[:, h, :])
            V_sync()
            V.tensor_copy(pos_f[:, :, :], pos_i[:, :, :])
            V.tensor_tensor(fin_d[:, :, :], fin[:, :, :], fin[:, :, 0:1].to_broadcast([T, HEADS, TOPK]),
                            ALU.subtract).then_inc(fin_d_ready, 1)
            V_sync()
            for c in range(0, HEADS, HH):
                V.tensor_tensor(onehot[:, :, :, :],
                                iota_cand[:, None, None, :].to_broadcast([T, HH, TOPK, CAND]),
                                pos_f[:, c:c + HH, :, None].to_broadcast([T, HH, TOPK, CAND]), ALU.is_equal)
                V_sync()
                V.tensor_tensor(onehot[:, :, :, :], onehot[:, :, :, :],
                                cand_i[:, c:c + HH, None, :].to_broadcast([T, HH, TOPK, CAND]), ALU.mult)
                V_sync()
                V.tensor_reduce(idx_f[:, c:c + HH, :], onehot[:, :, :, :], AX.X, ALU.add)
                V_sync()
            V.tensor_copy(idx[p][:, :], idx_f[:, :, :].rearrange("t h k -> t (h k)")).then_inc(idx_ready, 1)
            dve.wait_ge(fin_e_ready, b + 1)
            V.tensor_reduce(fin_s[:, :], fin_e[:, :, :], AX.X, ALU.add)
            V_sync()
            V.reciprocal(fin_r[:, :], fin_s[:, :])
            V_sync()
            V.tensor_tensor(kv_w[p][:, :, :], fin_e[:, :, :],
                            fin_r[:, :, None].to_broadcast([T, HEADS, TOPK]), ALU.mult).then_inc(kv_w_ready, 1)
            V_sync()

        def front(it, p):
            tokenizer(it, p)
            select(it, p)

        def attention(it, p):
            b = 2 * it + p
            dve.wait_ge(s_mm, b + 1)
            V.tensor_tensor(prob[:, :, :], p_y[:, :].rearrange("t (h j) -> t h j", h=HEADS),
                            causal[:, None, :].to_broadcast([T, HEADS, T]), ALU.add)
            V_sync()
            V.tensor_reduce(neg_max[:, :], prob[:, :, :], AX.X, ALU.max, negate=True).then_inc(neg_max_ready, 1)
            dve.wait_ge(prob_ready, b + 1)
            V.reciprocal(row_inv[:, :], row_sum[:, :])
            V_sync()
            dve.wait_ge(attn_mm, b + 1)
            V.tensor_tensor(attn_o[:, :].rearrange("t (h d) -> t h d", h=HEADS),
                            p_y[:, 0:512].rearrange("t (h d) -> t h d", h=HEADS),
                            row_inv[:, :, None].to_broadcast([T, HEADS, C]), ALU.mult).then_inc(attn_o_ready, 1)
            dve.wait_ge(wo_mm, b + 1)
            V.tensor_tensor(h2[:, :], h1[p][:, :], p_back[:, 0:C], ALU.add)
            V_sync()

        def linear_attention(it, p):
            b = 2 * it + p
            back_stats(h2[:, :], 1, b)
            normalise(xh3[:, :], h2[:, :], b_mv[:, 0:1], b_rstd[:, 0:1])
            V_sync()
            dve.sem_inc(xh3_ready, 1)
            dve.wait_ge(qkv_mm, b + 1)
            V.tensor_reduce(neg_kmax[:, :], p_back[0:C, 256:384], AX.X, ALU.max, negate=True
                            ).then_inc(neg_kmax_ready, 1)
            dve.wait_ge(ek_t_ready, b + 1)
            V.reciprocal(k_inv[:, :], k_sum[:, :])
            V_sync()
            dve.wait_ge(l1_a_mm, b + 1)
            V.scalar_tensor_tensor(l1_a[:, :], p_back[0:C, 128:192], k_inv[:, 0:1], block8[:, :], ALU.mult,
                                   ALU.mult).then_inc(l1_a_ready, 1)
            dve.wait_ge(l1_o_mm, b + 1)
            V.tensor_tensor(l1_x[:, :, :, :],
                            p_back[0:C, 256:384].rearrange("d (m j) -> d j m", j=L1_HEADS)[:, :, None, :]
                            .to_broadcast([C, L1_HEADS, L1_HEADS, T // L1_HEADS]),
                            block8[:, :].rearrange("d (h e) -> d h e", e=C // L1_HEADS)[:, None, :, 0:1]
                            .to_broadcast([C, L1_HEADS, L1_HEADS, T // L1_HEADS]), ALU.mult
                            ).then_inc(l1_x_ready, 1)
            dve.wait_ge(l1_mm, b + 1)
            V.tensor_tensor(z[:, :], p_back[:, 0:C], rc("bout"), ALU.add)
            V_sync()
            back_stats(z[:, :], 2, b)
            normalise(z[:, :], z[:, :], b_mv[:, 0:1], b_rstd[:, 0:1])
            V_sync()
            V.tensor_tensor(z[:, :], z[:, :], rc("l1_gamma"), ALU.mult)
            V_sync()
            V.tensor_tensor(z[:, :], z[:, :], rc("l1_beta"), ALU.add)
            V_sync()
            V.tensor_tensor(h3[:, :], h2[:, :], z[:, :], ALU.add)
            V_sync()

        def experts(it, p):
            b = 2 * it + p
            back_stats(h3[:, :], 3, b)
            normalise(xn[:, :], h3[:, :], b_mv[:, 0:1], b_rstd[:, 0:1])
            V_sync()
            back_stats(xn[:, :], 4, b)
            normalise(xn[:, :], xn[:, :], b_mv[:, 0:1], b_rstd[:, 0:1])
            V_sync()
            V.tensor_tensor(xn[:, :], xn[:, :], rc("ffn_gamma"), ALU.mult)
            V_sync()
            V.tensor_tensor(xn[:, :], xn[:, :], rc("ffn_beta"), ALU.add).then_inc(xn_ready, 1)
            dve.wait_ge(logit_mm, b + 1)
            V.tensor_tensor(logit[:, :], p_back[:, 192:192 + E], rc("br"), ALU.add)
            V_sync()
            V.max(best[:, :], logit[:, :])
            V_sync()
            V.max_index(best_i[:, :], best[:, :], logit[:, :])
            V.tensor_tensor(gap[:, :], best[:, 1:2], best[:, 0:1], ALU.subtract).then_inc(gap_ready, 1)
            V_sync()
            V.tensor_copy(best_f[:, :], best_i[:, 0:2])
            V_sync()
            dve.wait_ge(gap_e_ready, b + 1)
            V.tensor_scalar(gap_d[:, :], gap_e[:, :], 1.0, None, ALU.add)
            V_sync()
            V.reciprocal(mix[:, 0:1], gap_d[:, :])
            V_sync()
            V.tensor_tensor(mix[:, 1:2], mix[:, 0:1], gap_e[:, :], ALU.mult)
            V_sync()
            for j in range(2):
                V.tensor_scalar(pick[:, j, :], iota_e[:, :], best_f[:, j:j + 1], mix[:, j:j + 1],
                                ALU.is_equal, ALU.mult)
            V_sync()
            V.tensor_tensor(w_full[:, :], pick[:, 0, :], pick[:, 1, :], ALU.add)
            V_sync()
            dve.wait_ge(y_mm, b + 1)
            V.tensor_tensor(y_e[:, :, :], p_y[:, 0:512].rearrange("t (e c) -> t e c", e=E),
                            rc("b2").rearrange("t (e c) -> t e c", e=E), ALU.add)
            V_sync()
            V.tensor_tensor(y_e[:, :, :], y_e[:, :, :], w_full[:, :, None].to_broadcast([T, E, C]), ALU.mult)
            V_sync()
            V.tensor_reduce(y_sum[:, :], y_e[:, :, :].rearrange("t e c -> t c e"), AX.X, ALU.add)
            V_sync()
            dve.wait_ge(out_free[p], 16 * it + 16)
            V.tensor_tensor(h_out[p][:, :], h3[:, :], y_sum[:, :], ALU.add).then_inc(out_ready, 1)
            V_sync()

        def back(it, p):
            attention(it, p)
            linear_attention(it, p)
            experts(it, p)

        dve.wait_ge(consts_loaded, 16 * N_CONST_DMAS)
        dve.wait_ge(pool_consts, 8)
        over_batches(dve, front, back)

    @block.scalar
    def _(act):
        A = nc.scalar
        act.dma_start(w1_sb[:, :, :], w1).then_inc(consts_loaded, 16)
        act.dma_start(w2_sb[:, :, :], w2).then_inc(consts_loaded, 16)
        act.dma_start(b1_sb[:, :], b1_t).then_inc(consts_loaded, 16)
        A.preload_act_table_set("natural_log_exp_and_others")
        act.wait_ge(score_mm, 1)
        for c in range(2):
            last = A.copy(score_w[:, 512 * c:512 * c + 512], p_sim[0:C, 512 * c:512 * c + 512])
        last.then_inc(score_ready, 1)

        def root(var_sem, rstd_sem, count, var, log, rstd0):
            act.wait_ge(var_sem, count)
            A.activation(log[:, :], var[:, :], ACT.Ln)
            act.drain()
            A.activation(rstd0[:, :], log[:, :], ACT.Exp, scale=-0.5).then_inc(rstd_sem, 1)

        def front(it, p):
            b = 2 * it + p
            root(f_var_ready, f_rstd_ready, 3 * b + 1, f_var, f_log, f_rstd0)
            root(f_var_ready, f_rstd_ready, 3 * b + 2, f_var, f_log, f_rstd0)
            act.wait_ge(gram_mm, b + 1)
            A.copy(gram[:, :], p_front[0:C, 256:320])
            A.copy(xh1_t[:, :], p_front[0:C, 128:256]).then_inc(gram_ready, 1)
            act.wait_ge(attn_m_mm, b + 1)
            A.copy(attn_m[:, :], p_front[0:C, 320:384]).then_inc(attn_m_ready, 1)
            root(f_var_ready, f_rstd_ready, 3 * b + 3, f_var, f_log, f_rstd0)
            act.wait_ge(xh2_tr, b + 1)
            A.copy(xh2_t[p][:, :], p_front[0:C, 128:256]).then_inc(xh2_t_ready, 1)
            act.wait_ge(fin_d_ready, b + 1)
            A.activation(fin_e[:, :, :], fin_d[:, :, :], ACT.Exp).then_inc(fin_e_ready, 1)

        def back(it, p):
            b = 2 * it + p
            act.wait_ge(q_mm, b + 1)
            for c in range(2):
                last = A.activation(q_t[:, 4 * c:4 * c + 4, :].rearrange("d h t -> d (h t)"),
                                    p_x[0:C, 512 * c:512 * c + 512], ACT.Copy, scale=Q_SCALE)
            last.then_inc(q_ready, 1)
            for h in range(HEADS):
                if h == 0:
                    act.wait_ge(kv_w_ready, b + 1)
                act.wait_ge(gathered[p][h], 16 * TOPK * it + 16 * TOPK)
                for k in range(TOPK):
                    last = A.activation(gath[p][:, h, k, :], gath[p][:, h, k, :], ACT.Copy,
                                        scale=kv_w[p][:, h, k:k + 1])
                last.then_inc(scaled, 1)
            act.wait_ge(kv_mm, HEADS * b + HEADS)
            for c in range(2):
                last = A.copy(kv[:, 4 * c:4 * c + 4, :].rearrange("t h d -> t (h d)"),
                              p_y[:, 512 * c:512 * c + 512])
            last.then_inc(kv_ready, 1)
            act.wait_ge(k_tr, b + 1)
            for c in range(2):
                last = A.copy(k_t[:, 4 * c:4 * c + 4, :].rearrange("d h t -> d (h t)"),
                              p_x[0:C, 512 * c:512 * c + 512])
            last.then_inc(k_t_ready, 1)
            act.wait_ge(neg_max_ready, b + 1)
            for h in range(HEADS):
                last = A.activation(prob[:, h, :], prob[:, h, :], ACT.Exp, bias=neg_max[:, h:h + 1],
                                    accum_out=row_sum[:, h:h + 1])
            last.then_inc(prob_ready, 1)
            act.wait_ge(prob_tr, b + 1)
            for c in range(2):
                last = A.copy(prob_t[:, 4 * c:4 * c + 4, :].rearrange("j h i -> j (h i)"),
                              p_x[:, 512 * c:512 * c + 512])
            last.then_inc(prob_t_ready, 1)
            act.wait_ge(attn_o_tr, b + 1)
            A.copy(attn_o_t[:, :, :].rearrange("d c t -> d (c t)"), p_y[:, 512:1024]).then_inc(attn_o_t_ready, 1)
            root(b_var_ready, b_rstd_ready, 4 * b + 1, b_var, b_log, b_rstd0)
            act.wait_ge(xh3_tr, b + 1)
            A.copy(xh3_t[:, :], p_back[0:C, 64:192]).then_inc(xh3_t_ready, 1)
            act.wait_ge(neg_kmax_ready, b + 1)
            A.activation(l1_q[:, :], p_back[:, 192:256], ACT.Copy, scale=Q_SCALE)
            A.copy(l1_v_t[:, :], p_back[0:C, 384:512])
            A.activation(ek_t[:, :], p_back[0:C, 256:384], ACT.Exp, bias=neg_kmax[:, 0:1],
                         accum_out=k_sum[:, 0:1]).then_inc(ek_t_ready, 1)
            act.wait_ge(ek_tr, b + 1)
            A.copy(ek[:, :], p_back[:, 64:128]).then_inc(ek_ready, 1)
            root(b_var_ready, b_rstd_ready, 4 * b + 2, b_var, b_log, b_rstd0)
            root(b_var_ready, b_rstd_ready, 4 * b + 3, b_var, b_log, b_rstd0)
            root(b_var_ready, b_rstd_ready, 4 * b + 4, b_var, b_log, b_rstd0)
            act.wait_ge(xn_tr, b + 1)
            A.copy(xn_t[:, :], p_back[0:C, 64:192]).then_inc(xn_t_ready, 1)
            act.wait_ge(gap_ready, b + 1)
            A.activation(gap_e[:, :], gap[:, :], ACT.Exp).then_inc(gap_e_ready, 1)
            act.wait_ge(hid_mm, b + 1)
            for e in range(E):
                last = A.activation(hid[:, e, :], p_x[:, HID * e:HID * e + HID], ACT.Gelu, bias=b1_sb[:, e:e + 1])
            last.then_inc(hid_ready, 1)
            A.preload_act_table_set("natural_log_exp_and_others")

        over_batches(act, front, back)

    @block.tensor
    def _(pe):
        M = nc.tensor.matmul
        TR = nc.tensor.transpose

        pe.wait_ge(consts_loaded, 16 * N_CONST_DMAS)
        pe.wait_ge(pool_consts, 8)
        for g in range(GROUPS):
            last = M(p_sim[0:C, SUBKEYS * g:SUBKEYS * g + SUBKEYS], wqpk_sb[:, g, :], keys_sb[:, g, :],
                     start=True, stop=True)
        last.then_inc(score_mm, 1)
        pe.wait_ge(score_ready, 1)

        def front(it, p):
            b = 2 * it + p
            hold(pe, rowstats_ready, b + 1)
            M(p_front[:, 0:1], mean_w[:, :], rowstat[:, 0:1], start=True, stop=True).then_inc(mean_ready, 1)
            hold(pe, dev_ready, b + 1)
            M(p_front[:, 1:2], mean_w[:, :], dev_sq[:, :], start=True, stop=True).then_inc(var_ready, 1)
            hold(pe, xh1_ready, b + 1)
            TR(p_front[0:C, 128:256], xh1[:, :], ident[:, :])
            M(p_front[0:C, 256:320], xh1[:, :], xh1[:, :], start=True, stop=True).then_inc(gram_mm, 1)
            hold(pe, gram_ready, b + 1)
            M(p_front[0:C, 320:384], attn_w[:, :], gram[:, :], start=True, stop=True).then_inc(attn_m_mm, 1)
            hold(pe, attn_m_ready, b + 1)
            M(p_front[:, 384:448], xh1_t[:, :], attn_m[:, :], start=True, stop=True).then_inc(attn0_mm, 1)
            hold(pe, xh2_ready, b + 1)
            TR(p_front[0:C, 128:256], xh2[:, :], ident[:, :]).then_inc(xh2_tr, 1)
            hold(pe, xh2_t_ready, b + 1)
            for c in range(2):
                last = M(p_sim[:, 512 * c:512 * c + 512], xh2_t[p][:, :], score_w[:, 512 * c:512 * c + 512],
                         start=True, stop=True)
            last.then_inc(sim_mm, 1)

        def back(it, p):
            b = 2 * it + p
            for h in range(HEADS):
                last = M(p_x[0:C, T * h:T * h + T], wq_sb[:, C * h:C * h + C], xh2_t[p][:, :],
                         start=True, stop=True)
            last.then_inc(q_mm, 1)
            if isinstance(b, int) and b == B - 1:
                pe.wait_ge(out_ready, b)
            for h in range(HEADS):
                hold(pe, scaled, HEADS * b + h + 1)
                for k in range(TOPK):
                    last = M(p_y[:, KV * h:KV * h + KV], ident[:, :], gath[p][:, h, k, :],
                             start=(k == 0), stop=(k == TOPK - 1))
                last.then_inc(kv_mm, 1)
            hold(pe, kv_ready, b + 1)
            for h in range(HEADS):
                last = TR(p_x[0:C, T * h:T * h + T], kv[:, h, 0:C], ident[:, :])
            last.then_inc(k_tr, 1)
            hold(pe, q_ready, b + 1)
            hold(pe, k_t_ready, b + 1)
            for h in range(HEADS):
                last = M(p_y[:, T * h:T * h + T], q_t[:, h, :], k_t[:, h, :], start=True, stop=True)
            last.then_inc(s_mm, 1)
            hold(pe, prob_ready, b + 1)
            for h in range(HEADS):
                last = TR(p_x[:, T * h:T * h + T], prob[:, h, :], ident[:, :])
            last.then_inc(prob_tr, 1)
            hold(pe, prob_t_ready, b + 1)
            for h in range(HEADS):
                last = M(p_y[:, C * h:C * h + C], prob_t[:, h, :], kv[:, h, C:KV], start=True, stop=True)
            last.then_inc(attn_mm, 1)
            hold(pe, attn_o_ready, b + 1)
            for c in range(HEADS * C // 128):
                last = TR(p_y[:, 512 + T * c:512 + T * c + T], attn_o[:, 128 * c:128 * c + 128], ident[:, :])
            last.then_inc(attn_o_tr, 1)
            hold(pe, attn_o_t_ready, b + 1)
            n = HEADS * C // 128
            for c in range(n):
                last = M(p_back[:, 0:C], attn_o_t[:, c, :], wo_sb[:, c, :], start=(c == 0), stop=(c == n - 1))
            last.then_inc(wo_mm, 1)
            hold(pe, xh3_ready, b + 1)
            TR(p_back[0:C, 64:192], xh3[:, :], ident[:, :]).then_inc(xh3_tr, 1)
            hold(pe, xh3_t_ready, b + 1)
            M(p_back[:, 192:256], xh3_t[:, :], wqkv_sb[:, 0:C], start=True, stop=True)
            M(p_back[0:C, 256:384], wqkv_sb[:, C:2 * C], xh3_t[:, :], start=True, stop=True)
            M(p_back[0:C, 384:512], wqkv_sb[:, 2 * C:3 * C], xh3_t[:, :], start=True, stop=True
              ).then_inc(qkv_mm, 1)
            hold(pe, ek_t_ready, b + 1)
            TR(p_back[:, 64:128], ek_t[:, :], ident[0:C, 0:C]).then_inc(ek_tr, 1)
            hold(pe, ek_ready, b + 1)
            M(p_back[0:C, 128:192], ek[:, :], l1_q[:, :], start=True, stop=True).then_inc(l1_a_mm, 1)
            hold(pe, l1_a_ready, b + 1)
            M(p_back[0:C, 256:384], l1_a[:, :], l1_v_t[:, :], start=True, stop=True).then_inc(l1_o_mm, 1)
            hold(pe, l1_x_ready, b + 1)
            for j in range(L1_HEADS):
                last = M(p_back[:, 0:C], l1_x[:, j, :, :].rearrange("d h m -> d (h m)"), wout_sb[:, j, :],
                         start=(j == 0), stop=(j == L1_HEADS - 1))
            last.then_inc(l1_mm, 1)
            hold(pe, xn_ready, b + 1)
            TR(p_back[0:C, 64:192], xn[:, :], ident[:, :]).then_inc(xn_tr, 1)
            hold(pe, xn_t_ready, b + 1)
            M(p_back[:, 192:192 + E], xn_t[:, :], wr_sb[:, :], start=True, stop=True).then_inc(logit_mm, 1)
            for e in range(E):
                last = M(p_x[:, HID * e:HID * e + HID], w1_sb[:, e, :], xn_t[:, :], start=True, stop=True)
            last.then_inc(hid_mm, 1)
            hold(pe, hid_ready, b + 1)
            for e in range(E):
                last = M(p_y[:, C * e:C * e + C], hid[:, e, :], w2_sb[:, e, :], start=True, stop=True)
            last.then_inc(y_mm, 1)

        over_batches(pe, front, back)

    ctx.close()


def kernel(**inputs):
    import numpy as np
    import concourse.bacc as bacc
    from concourse.bass_utils import run_bass_kernel_spmd

    g = {k: np.asarray(v) for k, v in inputs.items()}
    spread = {"conv_w": g["L0_tok_w"], "conv_b": g["L0_tok_b"], "tok_gamma": g["L0_tok_gamma"],
              "tok_beta": g["L0_tok_beta"], "tok_alpha": g["L0_tok_alpha"], "bout": g["L1_attn_bout"],
              "l1_gamma": g["L1_attn_gamma"], "l1_beta": g["L1_attn_beta"], "ffn_gamma": g["L1_ffn_gamma"],
              "ffn_beta": g["L1_ffn_beta"], "br": g["L1_ffn_br"], "b2": g["L1_ffn_b2"]}
    rows = np.concatenate([spread[n].reshape(-1) for n in ROWS])
    arrays = {
        "x": g["x"],
        "rows": np.broadcast_to(rows[None, :], (T, ROW_WORDS)),
        "attn_w": g["L0_attn_W"],
        "wqpk_t": g["L0_ffn_Wq_pk"].reshape(C, GROUPS, DKEY).transpose(2, 1, 0),
        "keys_t": g["L0_ffn_pk_keys"].transpose(3, 0, 2, 1).reshape(DKEY, GROUPS, SUBKEYS),
        "wq": g["L0_ffn_Wq"],
        "table": np.concatenate([g["L0_ffn_keys_table"], g["L0_ffn_values_table"]], axis=1),
        "wo": g["L0_ffn_Wo"].reshape(-1, 128, C).transpose(1, 0, 2),
        "wqkv": g["L1_attn_Wqkv"],
        "wout": np.tile(g["L1_attn_Wout"].reshape(-1, C // L1_HEADS, C).transpose(1, 0, 2), (L1_HEADS, 1, 1)),
        "wr": g["L1_ffn_Wr"],
        "w1": g["L1_ffn_W1"].transpose(1, 0, 2),
        "b1_t": g["L1_ffn_b1"].transpose(1, 0),
        "w2": g["L1_ffn_W2"].transpose(1, 0, 2),
    }
    arrays = {k: np.ascontiguousarray(v) for k, v in arrays.items()}
    nc = bacc.Bacc("TRN2", target_bir_lowering=False, num_devices=1)
    args = [nc.dram_tensor(f"in_{k}", v.shape, F32, kind="ExternalInput").ap() for k, v in arrays.items()]
    out = nc.dram_tensor("out", (B, T, C), F32, kind="ExternalOutput").ap()
    build(nc, *args, out)
    r = run_bass_kernel_spmd(nc, [{f"in_{k}": v for k, v in arrays.items()}], core_ids=[0])
    return r.results[0]["out"]
```

```python
from contextlib import ExitStack

import concourse.bass as bass
from concourse import mybir

F32 = mybir.dt.float32
U32 = mybir.dt.uint32
I32 = mybir.dt.int32
ALU = mybir.AluOpType
ACT = mybir.ActivationFunctionType
AX = mybir.AxisListType

B, T_IN, C = 128, 256, 64
TAPS, STRIDE = 5, 2
T = T_IN // STRIDE
PAD_LOW = ((T - 1) * STRIDE + TAPS - T_IN) // 2
HEADS, SIDES, SUBKEYS, DKEY = 8, 2, 64, 32
GROUPS = SIDES * HEADS
TOPK = 16
KV = 2 * C
E, HID = 8, 128
L1_HEADS = 8
NEG = -3.0e38
EPS_TOK, EPS = 1e-3, 1e-5
Q_SCALE = C ** -0.5

SEGMENTS = []
_off = 0
for _r0, _rows in ((0, 1), (1, 1), (2, 1), (3, 1), (4, 1), (5, 3), (8, 8)):
    _w = TOPK // (_r0 + 1)
    SEGMENTS.append((_r0, _rows, _w, _off))
    _off += _rows * _w
CAND = _off

ROWS = {}
_at = 0
for _name, _n in (("conv_w", TAPS * C), ("conv_b", C), ("tok_gamma", C), ("tok_beta", C), ("tok_alpha", C),
                  ("bout", C), ("l1_gamma", C), ("l1_beta", C), ("ffn_gamma", C), ("ffn_beta", C),
                  ("br", E), ("b2", E * C)):
    ROWS[_name] = (_at, _at + _n)
    _at += _n
ROW_WORDS = _at
N_CONST_DMAS = 12


def build(nc, x, rows, w_mask_src, wqpk_t, keys_t, wq, table, wo, wqkv, wout, wr, w1, b1_t, w2, out):
    ctx = ExitStack()

    def sb(name, shape, dt=F32):
        return ctx.enter_context(nc.sbuf_tensor(name, shape, dt))

    def sem(name):
        return ctx.enter_context(nc.semaphore(name))

    def psum(name, shape):
        return ctx.enter_context(nc.psum_tensor(name, shape, F32))

    row = sb("row_consts", [T, ROW_WORDS])
    ident = sb("ident", [128, 128])
    mean_w = sb("mean_w", [128, 128])
    causal = sb("causal", [T, T])
    block8 = sb("block8", [C, C])
    iota_cand = sb("iota_cand", [T, CAND])
    iota_e = sb("iota_e", [T, E])
    table_base = sb("table_base", [T, HEADS])
    attn_w = sb("attn_w", [C, C])
    score_w = sb("score_w", [C, GROUPS * SUBKEYS])
    wq_sb = sb("wq_sb", [C, HEADS * C])
    wo_sb = sb("wo_sb", [128, HEADS * C // 128, C])
    wqkv_sb = sb("wqkv_sb", [C, 3 * C])
    wout_sb = sb("wout_sb", [C, L1_HEADS, C])
    wr_sb = sb("wr_sb", [C, E])
    w1_sb = sb("w1_sb", [C, E, HID])
    b1_sb = sb("b1_sb", [HID, E])
    w2_sb = sb("w2_sb", [HID, E, C])

    def rc(name):
        a, b = ROWS[name]
        return row[:, a:b]

    xwin = [sb(f"xwin{p}", [T, TAPS, C]) for p in range(2)]
    taps = sb("taps", [T, TAPS, C])
    y = sb("y", [T, C])
    stats6 = sb("stats6", [T, 6])
    rowstat = sb("rowstat", [T, 2])
    dev = sb("dev", [T, 1])
    dev_sq = sb("dev_sq", [T, 1])
    tok_mean = sb("tok_mean", [T, 1])
    f_var = sb("f_var", [T, 1])
    f_rstd0 = sb("f_rstd0", [T, 1])
    f_log = sb("f_log", [T, 1])
    f_tmp = sb("f_tmp", [T, 2])
    f_rstd = sb("f_rstd", [T, 1])
    yn, neg_part = taps[:, 0, :], taps[:, 1, :]
    h0 = sb("h0", [T, C])
    xh1 = sb("xh1", [T, C])
    xh1_t = sb("xh1_t", [C, T])
    gram = sb("gram", [C, C])
    attn_m = sb("attn_m", [C, C])
    h1 = [sb(f"h1_{p}", [T, C]) for p in range(2)]
    xh2 = sb("xh2", [T, C])
    xh2_t = [sb(f"xh2_t{p}", [C, T]) for p in range(2)]
    top = sb("top", [T, SIDES, HEADS, TOPK])
    top_i = sb("top_i", [T, SIDES, HEADS, TOPK], U32)
    top_f = sb("top_f", [T, SIDES, HEADS, TOPK])
    sim_rest = sb("sim_rest", [T, GROUPS, SUBKEYS])
    cand = sb("cand", [T, HEADS, CAND])
    cand_rest = sb("cand_rest", [T, HEADS, CAND])
    cand_i = sb("cand_i", [T, HEADS, CAND])
    fin = sb("fin", [T, HEADS, TOPK])
    pos_i = sb("pos_i", [T, HEADS, TOPK], U32)
    pos_f = sb("pos_f", [T, HEADS, TOPK])
    HH = HEADS // 4
    onehot = sb("onehot", [T, HH, TOPK, CAND])
    idx_f = sb("idx_f", [T, HEADS, TOPK])
    idx = [sb(f"idx{p}", [T, HEADS * TOPK], I32) for p in range(2)]
    fin_d = sb("fin_d", [T, HEADS, TOPK])
    fin_e = sb("fin_e", [T, HEADS, TOPK])
    fin_s = sb("fin_s", [T, HEADS])
    fin_r = sb("fin_r", [T, HEADS])
    kv_w = [sb(f"kv_w{p}", [T, HEADS, TOPK]) for p in range(2)]
    gath = [sb(f"gath{p}", [T, HEADS, TOPK, KV]) for p in range(2)]
    wqpk_sb = gath[1][0:DKEY, 0, 0:8, :].rearrange("d k c -> d (k c)").rearrange("d (g c) -> d g c", g=GROUPS)
    keys_sb = gath[1][0:DKEY, 1, 0:8, :].rearrange("d k c -> d (k c)").rearrange("d (g c) -> d g c", g=GROUPS)
    q_t = sb("q_t", [C, HEADS, T])
    kv = sb("kv", [T, HEADS, KV])
    k_t = sb("k_t", [C, HEADS, T])
    prob = sb("prob", [T, HEADS, T])
    neg_max = sb("neg_max", [T, HEADS])
    row_sum = sb("row_sum", [T, HEADS])
    row_inv = sb("row_inv", [T, HEADS])
    prob_t = sim_rest[:, :, :].rearrange("t g k -> t (g k)").rearrange("t (h i) -> t h i", h=HEADS)
    attn_o = sb("attn_o", [T, HEADS * C])
    attn_o_t = sb("attn_o_t", [128, HEADS * C // 128, T])
    b_stats6 = sb("b_stats6", [T, 6])
    b_mv = sb("b_mv", [T, 2])
    b_var = sb("b_var", [T, 1])
    b_rstd0 = sb("b_rstd0", [T, 1])
    b_log = sb("b_log", [T, 1])
    b_tmp = sb("b_tmp", [T, 2])
    b_rstd = sb("b_rstd", [T, 1])
    h2 = sb("h2", [T, C])
    xh3 = sb("xh3", [T, C])
    xh3_t = sb("xh3_t", [C, T])
    l1_q = sb("l1_q", [T, C])
    l1_v_t = sb("l1_v_t", [C, T])
    neg_kmax = sb("neg_kmax", [C, 1])
    ek_t = sb("ek_t", [C, T])
    k_sum = sb("k_sum", [C, 1])
    k_inv = sb("k_inv", [C, 1])
    ek = sb("ek", [T, C])
    l1_a = sb("l1_a", [C, C])
    l1_x = k_t[:, :, :].rearrange("d h t -> d (h t)").rearrange("d (j h m) -> d j h m", j=L1_HEADS, h=L1_HEADS)
    z = sb("z", [T, C])
    h3 = sb("h3", [T, C])
    xn = sb("xn", [T, C])
    xn_t = sb("xn_t", [C, T])
    logit = sb("logit", [T, E])
    best = sb("best", [T, 8])
    best_i = sb("best_i", [T, 8], U32)
    best_f = sb("best_f", [T, 2])
    gap = sb("gap", [T, 1])
    gap_e = sb("gap_e", [T, 1])
    gap_d = sb("gap_d", [T, 1])
    mix = sb("mix", [T, 2])
    pick = sb("pick", [T, 2, E])
    w_full = sb("w_full", [T, E])
    hid = prob
    y_e = attn_o[:, :].rearrange("t (e c) -> t e c", e=E)
    y_sum = sb("y_sum", [T, C])
    h_out = [sb(f"h_out{p}", [T, C]) for p in range(2)]

    p_front = psum("p_front", [128, 512])
    p_sim = psum("p_sim", [128, 1024])
    p_back = psum("p_back", [128, 512])
    p_x = psum("p_x", [128, 1024])
    p_y = psum("p_y", [128, 1024])

    consts_loaded = sem("consts_loaded")
    pool_consts = sem("pool_consts")
    pool_ones = sem("pool_ones")
    score_mm = sem("score_mm")
    score_ready = sem("score_ready")
    x_loaded = [sem(f"x_loaded{p}") for p in range(2)]
    conv_done = sem("conv_done")
    f_var_ready = sem("f_var_ready")
    f_rstd_ready = sem("f_rstd_ready")
    rowstats_ready = sem("rowstats_ready")
    mean_ready = sem("mean_ready")
    dev_ready = sem("dev_ready")
    var_ready = sem("var_ready")
    xh1_ready = sem("xh1_ready")
    gram_mm = sem("gram_mm")
    gram_ready = sem("gram_ready")
    attn_m_mm = sem("attn_m_mm")
    attn_m_ready = sem("attn_m_ready")
    attn0_mm = sem("attn0_mm")
    xh2_ready = sem("xh2_ready")
    xh2_tr = sem("xh2_tr")
    xh2_t_ready = sem("xh2_t_ready")
    sim_mm = sem("sim_mm")
    idx_ready = sem("idx_ready")
    fin_d_ready = sem("fin_d_ready")
    fin_e_ready = sem("fin_e_ready")
    kv_w_ready = sem("kv_w_ready")
    gathered = [[sem(f"gathered{p}_{h}") for h in range(HEADS)] for p in range(2)]
    scaled = sem("scaled")
    kv_mm = sem("kv_mm")
    kv_ready = sem("kv_ready")
    q_mm = sem("q_mm")
    q_ready = sem("q_ready")
    k_tr = sem("k_tr")
    k_t_ready = sem("k_t_ready")
    s_mm = sem("s_mm")
    neg_max_ready = sem("neg_max_ready")
    prob_ready = sem("prob_ready")
    prob_tr = sem("prob_tr")
    prob_t_ready = sem("prob_t_ready")
    attn_mm = sem("attn_mm")
    attn_o_ready = sem("attn_o_ready")
    attn_o_tr = sem("attn_o_tr")
    attn_o_t_ready = sem("attn_o_t_ready")
    wo_mm = sem("wo_mm")
    b_var_ready = sem("b_var_ready")
    b_rstd_ready = sem("b_rstd_ready")
    xh3_ready = sem("xh3_ready")
    xh3_tr = sem("xh3_tr")
    xh3_t_ready = sem("xh3_t_ready")
    qkv_mm = sem("qkv_mm")
    neg_kmax_ready = sem("neg_kmax_ready")
    ek_t_ready = sem("ek_t_ready")
    ek_tr = sem("ek_tr")
    ek_ready = sem("ek_ready")
    l1_a_mm = sem("l1_a_mm")
    l1_a_ready = sem("l1_a_ready")
    l1_o_mm = sem("l1_o_mm")
    l1_x_ready = sem("l1_x_ready")
    l1_mm = sem("l1_mm")
    xn_ready = sem("xn_ready")
    xn_tr = sem("xn_tr")
    xn_t_ready = sem("xn_t_ready")
    logit_mm = sem("logit_mm")
    gap_ready = sem("gap_ready")
    gap_e_ready = sem("gap_e_ready")
    hid_mm = sem("hid_mm")
    hid_ready = sem("hid_ready")
    y_mm = sem("y_mm")
    sums_free = sem("sums_free")
    out_ready = sem("out_ready")
    out_free = [sem(f"out_free{p}") for p in range(2)]

    waits_passed = sem("waits_passed")

    BUILT = 6

    def hold(eng, s, value):
        eng.wait_ge(s, value)
        eng.sem_inc(waits_passed, 1)

    EARLY = 7

    def over_batches(eng, tokens, select, back):
        tokens(0, 0)
        select(0, 0, None)
        tokens(0, 1)
        with eng.Fori(0, B // 2 - 1) as it:
            for p in range(2):
                select(it + (p + 1) // 2, 1 - p, (it, p))
                back(it, p, (it + 1, p))
        select(B // 2 - 1, 1, (B // 2 - 1, 0))
        back(B // 2 - 1, 0, None)
        back(B // 2 - 1, 1, None)

    block = ctx.enter_context(nc.Block())

    @block.sync
    def _(sp):
        for dst, src in ((row[:, :], rows), (attn_w[:, :], w_mask_src), (wqpk_sb[:, :, :], wqpk_t),
                         (keys_sb[:, :, :], keys_t), (wq_sb[:, :], wq), (wo_sb[:, :, :], wo),
                         (wqkv_sb[:, :], wqkv), (wout_sb[:, :, :], wout), (wr_sb[:, :], wr)):
            sp.dma_start(dst, src).then_inc(consts_loaded, 16)

        def load_window(it, p):
            b = 2 * it + p
            xb = x[b] if isinstance(b, int) else x[bass.ds(b, 1)].rearrange("o t c -> (o t) c")
            w = xwin[p]
            sp.dma_start(w[:, 1:3, :], xb.rearrange("(t k) c -> t k c", k=2)).then_inc(x_loaded[p], 16)
            sp.dma_start(w[1:T, 0, :], xb.rearrange("(t k) c -> t k c", k=2)[0:T - 1, 1, :]
                         ).then_inc(x_loaded[p], 16)
            sp.dma_start(w[0:T - 1, 3:5, :], xb.rearrange("(t k) c -> t k c", k=2)[1:T, :, :]
                         ).then_inc(x_loaded[p], 16)

        def store(it, p):
            b = 2 * it + p
            ob = out[b] if isinstance(b, int) else out[bass.ds(b, 1)].rearrange("o t c -> (o t) c")
            sp.wait_ge(out_ready, b + 1)
            sp.dma_start(ob, h_out[p][:, :]).then_inc(out_free[p], 16)

        sp.sem_inc(out_free[0], 16)
        sp.sem_inc(out_free[1], 16)
        sp.wait_ge(pool_ones, BUILT)
        load_window(0, 0)
        load_window(0, 1)
        for p in range(2):
            sp.wait_ge(conv_done, p + 1)
            load_window(1, p)
        with sp.Fori(0, B // 2 - 2) as it:
            for p in range(2):
                sp.wait_ge(conv_done, 2 * it + p + 3)
                load_window(it + 2, p)
                store(it, p)
        for it in (B // 2 - 2, B // 2 - 1):
            for p in range(2):
                store(it, p)
        for p in range(2):
            sp.wait_ge(out_free[p], 16 * (B // 2 + 1))

    @block.gpsimd
    def _(pool):
        nc.gpsimd.memset(ident[:, :], 0.0).then_inc(pool_ones, 1)
        nc.gpsimd.memset(causal[:, :], 0.0).then_inc(pool_ones, 1)
        nc.gpsimd.memset(block8[:, :], 1.0).then_inc(pool_ones, 1)
        nc.gpsimd.memset(mean_w[:, :], 1.0 / 128).then_inc(pool_ones, 1)
        for p in range(2):
            nc.gpsimd.memset(xwin[p][:, :, :].rearrange("t k c -> t (k c)"), 0.0).then_inc(pool_ones, 1)
        pool.wait_ge(pool_ones, BUILT)
        nc.gpsimd.affine_select(out=ident[:, :], in_=ident[:, :], pattern=[[-1, 128]], compare_op=ALU.not_equal,
                                fill=1.0, base=0, channel_multiplier=1).then_inc(pool_consts, 1)
        nc.gpsimd.affine_select(out=causal[:, :], in_=causal[:, :], pattern=[[-1, T]], compare_op=ALU.is_ge,
                                fill=NEG, base=0, channel_multiplier=1).then_inc(pool_consts, 1)
        b8 = block8[:, :].rearrange("r (g j) -> r g j", g=L1_HEADS)
        nc.gpsimd.affine_select(out=b8, in_=b8, pattern=[[-8, L1_HEADS], [0, 8]], compare_op=ALU.is_ge,
                                fill=0.0, base=0, channel_multiplier=1).then_inc(pool_consts, 1)
        pool.wait_ge(pool_consts, 3)
        nc.gpsimd.affine_select(out=b8, in_=b8, pattern=[[8, L1_HEADS], [0, 8]], compare_op=ALU.is_ge,
                                fill=0.0, base=7, channel_multiplier=-1).then_inc(pool_consts, 1)
        nc.gpsimd.iota(iota_cand[:, :], pattern=[[1, CAND]], base=0, channel_multiplier=0,
                       allow_small_or_imprecise_dtypes=True).then_inc(pool_consts, 1)
        nc.gpsimd.iota(iota_e[:, :], pattern=[[1, E]], base=0, channel_multiplier=0,
                       allow_small_or_imprecise_dtypes=True).then_inc(pool_consts, 1)
        nc.gpsimd.iota(table_base[:, :], pattern=[[SUBKEYS * SUBKEYS, HEADS]], base=0, channel_multiplier=0,
                       allow_small_or_imprecise_dtypes=True).then_inc(pool_consts, 1)
        pool.wait_ge(consts_loaded, 16 * N_CONST_DMAS)
        nc.gpsimd.affine_select(out=attn_w[:, :], in_=attn_w[:, :], pattern=[[1, C]], compare_op=ALU.is_gt,
                                fill=0.0, base=0, channel_multiplier=-1).then_inc(pool_consts, 1)

        def gather(it, p):
            hold(pool, idx_ready, 2 * it + p + 1)
            for h in range(HEADS):
                for k in range(TOPK):
                    c = h * TOPK + k
                    nc.gpsimd.indirect_dma_start(
                        out=gath[p][:, h, k, :], out_offset=None, in_=table[:, :],
                        in_offset=bass.IndirectOffsetOnAxis(ap=idx[p][:, c:c + 1], axis=0),
                    ).then_inc(gathered[p][h], 16)

        with pool.Fori(0, B // 2) as it:
            for p in range(2):
                gather(it, p)

    @block.vector
    def _(dve):
        V = nc.vector
        V_sync = dve.drain

        def normalise(dst, src, mean, rstd):
            return V.tensor_scalar(dst, src, mean, rstd, ALU.subtract, ALU.mult)

        def newton(var, r0, tmp, dst):
            V.scalar_tensor_tensor(tmp[:, 0:1], r0[:, :], r0[:, 0:1], var[:, :], ALU.mult, ALU.mult)
            V_sync()
            V.tensor_scalar(tmp[:, 1:2], tmp[:, 0:1], -0.5, 1.5, ALU.mult, ALU.add)
            V_sync()
            V.tensor_tensor(dst[:, :], r0[:, :], tmp[:, 1:2], ALU.mult)
            V_sync()

        def front_var(src):
            V.bn_stats(stats6[:, :], src)
            V_sync()
            V.bn_aggr(rowstat[:, :], stats6[:, :])
            V_sync()
            V.tensor_scalar(f_var[:, :], rowstat[:, 1:2], EPS, None, ALU.add).then_inc(f_var_ready, 1)

        def front_norm(dst, src, count, ready):
            dve.wait_ge(f_rstd_ready, count)
            newton(f_var, f_rstd0, f_tmp, f_rstd)
            normalise(dst, src, rowstat[:, 0:1], f_rstd[:, 0:1]).then_inc(ready, 1)
            V_sync()

        def back_var(src):
            V.bn_stats(b_stats6[:, :], src)
            V_sync()
            V.bn_aggr(b_mv[:, :], b_stats6[:, :])
            V_sync()
            V.tensor_scalar(b_var[:, :], b_mv[:, 1:2], EPS, None, ALU.add).then_inc(b_var_ready, 1)

        def back_norm(dst, src, count):
            dve.wait_ge(b_rstd_ready, count)
            newton(b_var, b_rstd0, b_tmp, b_rstd)
            last = normalise(dst, src, b_mv[:, 0:1], b_rstd[:, 0:1])
            V_sync()
            return last

        def conv(it, p):
            dve.wait_ge(x_loaded[p], 48 * it + 48)
            V.tensor_tensor(taps[:, :, :], xwin[p][:, :, :],
                            rc("conv_w").rearrange("t (k c) -> t k c", k=TAPS), ALU.mult).then_inc(conv_done, 1)
            V_sync()
            V.tensor_reduce(y[:, :], taps[:, :, :].rearrange("t k c -> t c k"), AX.X, ALU.add)
            V_sync()
            V.tensor_tensor(y[:, :], y[:, :], rc("conv_b"), ALU.add)
            V_sync()
            V.bn_stats(stats6[:, :], y[:, :])
            V_sync()
            V.bn_aggr(rowstat[:, :], stats6[:, :]).then_inc(rowstats_ready, 1)

        def deviation(it, p):
            V_sync()
            dve.wait_ge(mean_ready, 2 * it + p + 1)
            V.tensor_copy(tok_mean[:, :], p_front[:, 0:1])
            V_sync()
            V.tensor_tensor(dev[:, :], rowstat[:, 0:1], tok_mean[:, :], ALU.subtract)
            V_sync()
            V.scalar_tensor_tensor(dev_sq[:, :], dev[:, :], dev[:, 0:1], rowstat[:, 1:2], ALU.mult,
                                   ALU.add).then_inc(dev_ready, 1)

        def variance(it, p):
            dve.wait_ge(var_ready, 2 * it + p + 1)
            V.tensor_scalar(f_var[:, :], p_front[:, 1:2], EPS_TOK, None, ALU.add).then_inc(f_var_ready, 1)

        def prelu(it, p):
            b = 2 * it + p
            dve.wait_ge(f_rstd_ready, 3 * b + 1)
            newton(f_var, f_rstd0, f_tmp, f_rstd)
            normalise(yn, y[:, :], tok_mean[:, 0:1], f_rstd[:, 0:1])
            V_sync()
            V.tensor_tensor(yn, yn, rc("tok_gamma"), ALU.mult)
            V_sync()
            V.tensor_tensor(yn, yn, rc("tok_beta"), ALU.add)
            V_sync()
            V.scalar_tensor_tensor(neg_part, yn, 0.0, rc("tok_alpha"), ALU.min, ALU.mult)
            V_sync()
            V.scalar_tensor_tensor(h0[:, :], yn, 0.0, neg_part, ALU.max, ALU.add)
            V_sync()
            front_var(h0[:, :])

        def norm1(it, p):
            front_norm(xh1[:, :], h0[:, :], 3 * (2 * it + p) + 2, xh1_ready)

        def add_attn0(it, p):
            dve.wait_ge(attn0_mm, 2 * it + p + 1)
            V.tensor_tensor(h1[p][:, :], h0[:, :], p_front[:, 384:448], ALU.add)
            V_sync()
            front_var(h1[p][:, :])

        def norm2(it, p):
            front_norm(xh2[:, :], h1[p][:, :], 3 * (2 * it + p) + 3, xh2_ready)

        def tokens(it, p):
            for step in (conv, deviation, variance, prelu, norm1, add_attn0, norm2):
                step(it, p)

        def select(it, p, before):
            b = 2 * it + p
            hold(dve, sim_mm, b + 1)
            sim = p_sim[:, :].rearrange("t (g k) -> t g k", g=GROUPS)
            tops = top[:, :, :, :].rearrange("t s h k -> t (s h) k")
            tops_i = top_i[:, :, :, :].rearrange("t s h k -> t (s h) k")
            for g in range(GROUPS):
                V.max(tops[:, g, 0:8], sim[:, g, :])
            V_sync()
            for g in range(GROUPS):
                V.max_index(tops_i[:, g, 0:8], tops[:, g, 0:8], sim[:, g, :])
                V.match_replace(sim_rest[:, g, :], tops[:, g, 0:8], sim[:, g, :], NEG)
            V_sync()
            for g in range(GROUPS):
                V.max(tops[:, g, 8:16], sim_rest[:, g, :])
            V_sync()
            for g in range(GROUPS):
                V.max_index(tops_i[:, g, 8:16], tops[:, g, 8:16], sim_rest[:, g, :])
            V_sync()
            V.tensor_tensor(top_f[:, 0], top_i[:, 0], table_base[:, :, None].to_broadcast([T, HEADS, TOPK]),
                            ALU.add)
            V.tensor_scalar(top_f[:, 1], top_i[:, 1], float(SUBKEYS), None, ALU.mult)
            V_sync()
            for src, dst in ((top, cand), (top_f, cand_i)):
                for r0, n, w, off in SEGMENTS:
                    o = dst[:, :, off:off + n * w].rearrange("t h (r c) -> t h r c", r=n)
                    a = src[:, 0, :, r0:r0 + n, None].to_broadcast([T, HEADS, n, w])
                    c = src[:, 1, :, None, 0:w].to_broadcast([T, HEADS, n, w])
                    V.tensor_tensor(o, a, c, ALU.add)
            V_sync()
            for h in range(HEADS):
                V.max(fin[:, h, 0:8], cand[:, h, :])
            V_sync()
            for h in range(HEADS):
                V.max_index(pos_i[:, h, 0:8], fin[:, h, 0:8], cand[:, h, :])
                V.match_replace(cand_rest[:, h, :], fin[:, h, 0:8], cand[:, h, :], NEG)
            V_sync()
            for h in range(HEADS):
                V.max(fin[:, h, 8:16], cand_rest[:, h, :])
            V_sync()
            for h in range(HEADS):
                V.max_index(pos_i[:, h, 8:16], fin[:, h, 8:16], cand_rest[:, h, :])
            V_sync()
            V.tensor_copy(pos_f[:, :, :], pos_i[:, :, :])
            V.tensor_tensor(fin_d[:, :, :], fin[:, :, :], fin[:, :, 0:1].to_broadcast([T, HEADS, TOPK]),
                            ALU.subtract).then_inc(fin_d_ready, 1)
            V_sync()
            for c in range(0, HEADS, HH):
                V.tensor_tensor(onehot[:, :, :, :],
                                iota_cand[:, None, None, :].to_broadcast([T, HH, TOPK, CAND]),
                                pos_f[:, c:c + HH, :, None].to_broadcast([T, HH, TOPK, CAND]), ALU.is_equal)
                V_sync()
                V.tensor_tensor(onehot[:, :, :, :], onehot[:, :, :, :],
                                cand_i[:, c:c + HH, None, :].to_broadcast([T, HH, TOPK, CAND]), ALU.mult)
                V_sync()
                V.tensor_reduce(idx_f[:, c:c + HH, :], onehot[:, :, :, :], AX.X, ALU.add)
                V_sync()
            V.tensor_copy(idx[p][:, :], idx_f[:, :, :].rearrange("t h k -> t (h k)")).then_inc(idx_ready, 1)
            dve.wait_ge(fin_e_ready, b + 1)
            V.tensor_reduce(fin_s[:, :], fin_e[:, :, :], AX.X, ALU.add)
            V_sync()
            V.reciprocal(fin_r[:, :], fin_s[:, :])
            V_sync()
            V.tensor_tensor(kv_w[p][:, :, :], fin_e[:, :, :],
                            fin_r[:, :, None].to_broadcast([T, HEADS, TOPK]), ALU.mult).then_inc(kv_w_ready, 1)
            V_sync()

        def back(it, p, ahead):
            b = 2 * it + p
            dve.wait_ge(s_mm, b + 1)
            V.tensor_tensor(prob[:, :, :], p_y[:, :].rearrange("t (h j) -> t h j", h=HEADS),
                            causal[:, None, :].to_broadcast([T, HEADS, T]), ALU.add)
            V_sync()
            V.tensor_reduce(neg_max[:, :], prob[:, :, :], AX.X, ALU.max, negate=True).then_inc(neg_max_ready, 1)
            if ahead is not None:
                conv(*ahead)
                deviation(*ahead)
                variance(*ahead)
            dve.wait_ge(prob_ready, b + 1)
            V.reciprocal(row_inv[:, :], row_sum[:, :])
            V_sync()
            if ahead is not None:
                prelu(*ahead)
            dve.wait_ge(attn_mm, b + 1)
            V.tensor_tensor(attn_o[:, :].rearrange("t (h d) -> t h d", h=HEADS),
                            p_y[:, 0:512].rearrange("t (h d) -> t h d", h=HEADS),
                            row_inv[:, :, None].to_broadcast([T, HEADS, C]), ALU.mult).then_inc(attn_o_ready, 1)
            if ahead is not None:
                norm1(*ahead)
            dve.wait_ge(wo_mm, b + 1)
            V.tensor_tensor(h2[:, :], h1[p][:, :], p_back[:, 0:C], ALU.add)
            V_sync()
            back_var(h2[:, :])
            back_norm(xh3[:, :], h2[:, :], 4 * b + 1)
            dve.sem_inc(xh3_ready, 1)
            if ahead is not None:
                add_attn0(*ahead)
            dve.wait_ge(qkv_mm, b + 1)
            V.tensor_reduce(neg_kmax[:, :], p_back[0:C, 256:384], AX.X, ALU.max, negate=True
                            ).then_inc(neg_kmax_ready, 1)
            if ahead is not None:
                norm2(*ahead)
            dve.wait_ge(ek_t_ready, b + 1)
            V.reciprocal(k_inv[:, :], k_sum[:, :])
            V_sync()
            dve.wait_ge(l1_a_mm, b + 1)
            V.scalar_tensor_tensor(l1_a[:, :], p_back[0:C, 128:192], k_inv[:, 0:1], block8[:, :], ALU.mult,
                                   ALU.mult).then_inc(l1_a_ready, 1)
            dve.wait_ge(l1_o_mm, b + 1)
            V.tensor_tensor(l1_x[:, :, :, :],
                            p_back[0:C, 256:384].rearrange("d (m j) -> d j m", j=L1_HEADS)[:, :, None, :]
                            .to_broadcast([C, L1_HEADS, L1_HEADS, T // L1_HEADS]),
                            block8[:, :].rearrange("d (h e) -> d h e", e=C // L1_HEADS)[:, None, :, 0:1]
                            .to_broadcast([C, L1_HEADS, L1_HEADS, T // L1_HEADS]), ALU.mult
                            ).then_inc(l1_x_ready, 1)
            dve.wait_ge(l1_mm, b + 1)
            V.tensor_tensor(z[:, :], p_back[:, 0:C], rc("bout"), ALU.add)
            V_sync()
            back_var(z[:, :])
            back_norm(z[:, :], z[:, :], 4 * b + 2)
            V.tensor_tensor(z[:, :], z[:, :], rc("l1_gamma"), ALU.mult)
            V_sync()
            V.tensor_tensor(z[:, :], z[:, :], rc("l1_beta"), ALU.add)
            V_sync()
            V.tensor_tensor(h3[:, :], h2[:, :], z[:, :], ALU.add)
            V_sync()
            back_var(h3[:, :])
            back_norm(xn[:, :], h3[:, :], 4 * b + 3)
            back_var(xn[:, :])
            back_norm(xn[:, :], xn[:, :], 4 * b + 4)
            V.tensor_tensor(xn[:, :], xn[:, :], rc("ffn_gamma"), ALU.mult)
            V_sync()
            V.tensor_tensor(xn[:, :], xn[:, :], rc("ffn_beta"), ALU.add).then_inc(xn_ready, 1)
            dve.wait_ge(logit_mm, b + 1)
            V.tensor_tensor(logit[:, :], p_back[:, 192:192 + E], rc("br"), ALU.add)
            V_sync()
            V.max(best[:, :], logit[:, :])
            V_sync()
            V.max_index(best_i[:, :], best[:, :], logit[:, :])
            V.tensor_tensor(gap[:, :], best[:, 1:2], best[:, 0:1], ALU.subtract).then_inc(gap_ready, 1)
            V_sync()
            V.tensor_copy(best_f[:, :], best_i[:, 0:2])
            V_sync()
            dve.wait_ge(gap_e_ready, b + 1)
            V.tensor_scalar(gap_d[:, :], gap_e[:, :], 1.0, None, ALU.add)
            V_sync()
            V.reciprocal(mix[:, 0:1], gap_d[:, :])
            V_sync()
            V.tensor_tensor(mix[:, 1:2], mix[:, 0:1], gap_e[:, :], ALU.mult)
            V_sync()
            for j in range(2):
                V.tensor_scalar(pick[:, j, :], iota_e[:, :], best_f[:, j:j + 1], mix[:, j:j + 1],
                                ALU.is_equal, ALU.mult)
            V_sync()
            V.tensor_tensor(w_full[:, :], pick[:, 0, :], pick[:, 1, :], ALU.add)
            V_sync()
            dve.wait_ge(y_mm, b + 1)
            V.tensor_tensor(y_e[:, :, :], p_y[:, 0:512].rearrange("t (e c) -> t e c", e=E),
                            rc("b2").rearrange("t (e c) -> t e c", e=E), ALU.add).then_inc(sums_free, 1)
            V_sync()
            V.tensor_tensor(y_e[:, :, :], y_e[:, :, :], w_full[:, :, None].to_broadcast([T, E, C]), ALU.mult)
            V_sync()
            V.tensor_reduce(y_sum[:, :], y_e[:, :, :].rearrange("t e c -> t c e"), AX.X, ALU.add)
            V_sync()
            dve.wait_ge(out_free[p], 16 * it + 16)
            V.tensor_tensor(h_out[p][:, :], h3[:, :], y_sum[:, :], ALU.add).then_inc(out_ready, 1)
            V_sync()

        dve.sem_inc(sums_free, 1)
        dve.wait_ge(consts_loaded, 16 * N_CONST_DMAS)
        dve.wait_ge(pool_consts, 8)
        over_batches(dve, tokens, select, back)

    @block.scalar
    def _(act):
        A = nc.scalar
        act.dma_start(w1_sb[:, :, :], w1).then_inc(consts_loaded, 16)
        act.dma_start(w2_sb[:, :, :], w2).then_inc(consts_loaded, 16)
        act.dma_start(b1_sb[:, :], b1_t).then_inc(consts_loaded, 16)
        A.preload_act_table_set("natural_log_exp_and_others")
        act.wait_ge(score_mm, 1)
        for c in range(2):
            last = A.copy(score_w[:, 512 * c:512 * c + 512], p_sim[0:C, 512 * c:512 * c + 512])
        last.then_inc(score_ready, 1)

        def root(var_sem, rstd_sem, count, var, log, rstd0):
            act.wait_ge(var_sem, count)
            A.activation(log[:, :], var[:, :], ACT.Ln)
            act.drain()
            A.activation(rstd0[:, :], log[:, :], ACT.Exp, scale=-0.5).then_inc(rstd_sem, 1)

        def queries(it, p):
            act.wait_ge(q_mm, 2 * it + p + 1)
            for c in range(2):
                last = A.activation(q_t[:, 4 * c:4 * c + 4, :].rearrange("d h t -> d (h t)"),
                                    p_x[0:C, 512 * c:512 * c + 512], ACT.Copy, scale=Q_SCALE)
            last.then_inc(q_ready, 1)

        def weigh(it, p, first, end):
            act.wait_ge(kv_w_ready, 2 * it + p + 1)
            for h in range(first, end):
                act.wait_ge(gathered[p][h], 16 * TOPK * it + 16 * TOPK)
                for k in range(TOPK):
                    last = A.activation(gath[p][:, h, k, :], gath[p][:, h, k, :], ACT.Copy,
                                        scale=kv_w[p][:, h, k:k + 1])
                last.then_inc(scaled, 1)

        def front_root(it, p, nth):
            root(f_var_ready, f_rstd_ready, 3 * (2 * it + p) + nth, f_var, f_log, f_rstd0)

        def gram_copies(it, p):
            act.wait_ge(gram_mm, 2 * it + p + 1)
            A.copy(gram[:, :], p_front[0:C, 256:320])
            A.copy(xh1_t[:, :], p_front[0:C, 128:256]).then_inc(gram_ready, 1)

        def attn_m_copy(it, p):
            act.wait_ge(attn_m_mm, 2 * it + p + 1)
            A.copy(attn_m[:, :], p_front[0:C, 320:384]).then_inc(attn_m_ready, 1)

        def xh2_copy(it, p):
            act.wait_ge(xh2_tr, 2 * it + p + 1)
            A.copy(xh2_t[p][:, :], p_front[0:C, 128:256]).then_inc(xh2_t_ready, 1)

        def tokens(it, p):
            front_root(it, p, 1)
            front_root(it, p, 2)
            gram_copies(it, p)
            attn_m_copy(it, p)
            front_root(it, p, 3)
            xh2_copy(it, p)

        def select(it, p, before):
            if before is not None:
                queries(*before)
                weigh(*before, 0, EARLY)
            act.wait_ge(fin_d_ready, 2 * it + p + 1)
            A.activation(fin_e[:, :, :], fin_d[:, :, :], ACT.Exp).then_inc(fin_e_ready, 1)

        def back(it, p, ahead):
            b = 2 * it + p
            last_batch = isinstance(b, int) and b == B - 1
            if last_batch:
                queries(it, p)
            weigh(it, p, 0 if last_batch else EARLY, HEADS)
            act.wait_ge(kv_mm, HEADS * b + HEADS)
            for c in range(2):
                last = A.copy(kv[:, 4 * c:4 * c + 4, :].rearrange("t h d -> t (h d)"),
                              p_y[:, 512 * c:512 * c + 512])
            last.then_inc(kv_ready, 1)
            act.wait_ge(k_tr, b + 1)
            for c in range(2):
                last = A.copy(k_t[:, 4 * c:4 * c + 4, :].rearrange("d h t -> d (h t)"),
                              p_x[0:C, 512 * c:512 * c + 512])
            last.then_inc(k_t_ready, 1)
            act.wait_ge(neg_max_ready, b + 1)
            for h in range(HEADS):
                last = A.activation(prob[:, h, :], prob[:, h, :], ACT.Exp, bias=neg_max[:, h:h + 1],
                                    accum_out=row_sum[:, h:h + 1])
            last.then_inc(prob_ready, 1)
            if ahead is not None:
                front_root(*ahead, 1)
            act.wait_ge(prob_tr, b + 1)
            for c in range(2):
                last = A.copy(prob_t[:, 4 * c:4 * c + 4, :].rearrange("j h i -> j (h i)"),
                              p_x[:, 512 * c:512 * c + 512])
            last.then_inc(prob_t_ready, 1)
            if ahead is not None:
                front_root(*ahead, 2)
            act.wait_ge(attn_o_tr, b + 1)
            A.copy(attn_o_t[:, :, :].rearrange("d c t -> d (c t)"), p_y[:, 512:1024]).then_inc(attn_o_t_ready, 1)
            if ahead is not None:
                gram_copies(*ahead)
            root(b_var_ready, b_rstd_ready, 4 * b + 1, b_var, b_log, b_rstd0)
            if ahead is not None:
                attn_m_copy(*ahead)
            act.wait_ge(xh3_tr, b + 1)
            A.copy(xh3_t[:, :], p_back[0:C, 64:192]).then_inc(xh3_t_ready, 1)
            if ahead is not None:
                front_root(*ahead, 3)
            act.wait_ge(neg_kmax_ready, b + 1)
            A.activation(l1_q[:, :], p_back[:, 192:256], ACT.Copy, scale=Q_SCALE)
            A.copy(l1_v_t[:, :], p_back[0:C, 384:512])
            A.activation(ek_t[:, :], p_back[0:C, 256:384], ACT.Exp, bias=neg_kmax[:, 0:1],
                         accum_out=k_sum[:, 0:1]).then_inc(ek_t_ready, 1)
            act.wait_ge(ek_tr, b + 1)
            A.copy(ek[:, :], p_back[:, 64:128]).then_inc(ek_ready, 1)
            if ahead is not None:
                xh2_copy(*ahead)
            root(b_var_ready, b_rstd_ready, 4 * b + 2, b_var, b_log, b_rstd0)
            root(b_var_ready, b_rstd_ready, 4 * b + 3, b_var, b_log, b_rstd0)
            root(b_var_ready, b_rstd_ready, 4 * b + 4, b_var, b_log, b_rstd0)
            act.wait_ge(xn_tr, b + 1)
            A.copy(xn_t[:, :], p_back[0:C, 64:192]).then_inc(xn_t_ready, 1)
            act.wait_ge(gap_ready, b + 1)
            A.activation(gap_e[:, :], gap[:, :], ACT.Exp).then_inc(gap_e_ready, 1)
            act.wait_ge(hid_mm, b + 1)
            for e in range(E):
                last = A.activation(hid[:, e, :], p_x[:, HID * e:HID * e + HID], ACT.Gelu, bias=b1_sb[:, e:e + 1])
            last.then_inc(hid_ready, 1)
            A.preload_act_table_set("natural_log_exp_and_others")

        over_batches(act, tokens, select, back)

    @block.tensor
    def _(pe):
        M = nc.tensor.matmul
        TR = nc.tensor.transpose

        pe.wait_ge(consts_loaded, 16 * N_CONST_DMAS)
        pe.wait_ge(pool_consts, 8)
        for g in range(GROUPS):
            last = M(p_sim[0:C, SUBKEYS * g:SUBKEYS * g + SUBKEYS], wqpk_sb[:, g, :], keys_sb[:, g, :],
                     start=True, stop=True)
        last.then_inc(score_mm, 1)
        pe.wait_ge(score_ready, 1)

        def queries(it, p):
            for h in range(HEADS):
                last = M(p_x[0:C, T * h:T * h + T], wq_sb[:, C * h:C * h + C], xh2_t[p][:, :],
                         start=True, stop=True)
            last.then_inc(q_mm, 1)

        def sum_rows(it, p, first, end):
            if first == 0:
                hold(pe, sums_free, 2 * it + p + 1)
            for h in range(first, end):
                hold(pe, scaled, HEADS * (2 * it + p) + h + 1)
                for k in range(TOPK):
                    last = M(p_y[:, KV * h:KV * h + KV], ident[:, :], gath[p][:, h, k, :],
                             start=(k == 0), stop=(k == TOPK - 1))
                last.then_inc(kv_mm, 1)

        def mean(it, p):
            hold(pe, rowstats_ready, 2 * it + p + 1)
            M(p_front[:, 0:1], mean_w[:, :], rowstat[:, 0:1], start=True, stop=True).then_inc(mean_ready, 1)

        def variance(it, p):
            hold(pe, dev_ready, 2 * it + p + 1)
            M(p_front[:, 1:2], mean_w[:, :], dev_sq[:, :], start=True, stop=True).then_inc(var_ready, 1)

        def gram_product(it, p):
            hold(pe, xh1_ready, 2 * it + p + 1)
            TR(p_front[0:C, 128:256], xh1[:, :], ident[:, :])
            M(p_front[0:C, 256:320], xh1[:, :], xh1[:, :], start=True, stop=True).then_inc(gram_mm, 1)

        def attn_m_product(it, p):
            hold(pe, gram_ready, 2 * it + p + 1)
            M(p_front[0:C, 320:384], attn_w[:, :], gram[:, :], start=True, stop=True).then_inc(attn_m_mm, 1)

        def attn0_product(it, p):
            hold(pe, attn_m_ready, 2 * it + p + 1)
            M(p_front[:, 384:448], xh1_t[:, :], attn_m[:, :], start=True, stop=True).then_inc(attn0_mm, 1)

        def xh2_transpose(it, p):
            hold(pe, xh2_ready, 2 * it + p + 1)
            TR(p_front[0:C, 128:256], xh2[:, :], ident[:, :]).then_inc(xh2_tr, 1)

        def scores(it, p):
            hold(pe, xh2_t_ready, 2 * it + p + 1)
            for c in range(2):
                last = M(p_sim[:, 512 * c:512 * c + 512], xh2_t[p][:, :], score_w[:, 512 * c:512 * c + 512],
                         start=True, stop=True)
            last.then_inc(sim_mm, 1)

        def tokens(it, p):
            for step in (mean, variance, gram_product, attn_m_product, attn0_product, xh2_transpose, scores):
                step(it, p)

        def select(it, p, before):
            if before is not None:
                queries(*before)
                sum_rows(*before, 0, EARLY)

        def back(it, p, ahead):
            b = 2 * it + p
            last_batch = isinstance(b, int) and b == B - 1
            if last_batch:
                queries(it, p)
            sum_rows(it, p, 0 if last_batch else EARLY, HEADS)
            hold(pe, kv_ready, b + 1)
            for h in range(HEADS):
                last = TR(p_x[0:C, T * h:T * h + T], kv[:, h, 0:C], ident[:, :])
            last.then_inc(k_tr, 1)
            hold(pe, q_ready, b + 1)
            hold(pe, k_t_ready, b + 1)
            for h in range(HEADS):
                last = M(p_y[:, T * h:T * h + T], q_t[:, h, :], k_t[:, h, :], start=True, stop=True)
            last.then_inc(s_mm, 1)
            if ahead is not None:
                mean(*ahead)
                variance(*ahead)
            hold(pe, prob_ready, b + 1)
            for h in range(HEADS):
                last = TR(p_x[:, T * h:T * h + T], prob[:, h, :], ident[:, :])
            last.then_inc(prob_tr, 1)
            hold(pe, prob_t_ready, b + 1)
            for h in range(HEADS):
                last = M(p_y[:, C * h:C * h + C], prob_t[:, h, :], kv[:, h, C:KV], start=True, stop=True)
            last.then_inc(attn_mm, 1)
            hold(pe, attn_o_ready, b + 1)
            for c in range(HEADS * C // 128):
                last = TR(p_y[:, 512 + T * c:512 + T * c + T], attn_o[:, 128 * c:128 * c + 128], ident[:, :])
            last.then_inc(attn_o_tr, 1)
            if ahead is not None:
                gram_product(*ahead)
            hold(pe, attn_o_t_ready, b + 1)
            n = HEADS * C // 128
            for c in range(n):
                last = M(p_back[:, 0:C], attn_o_t[:, c, :], wo_sb[:, c, :], start=(c == 0), stop=(c == n - 1))
            last.then_inc(wo_mm, 1)
            if ahead is not None:
                attn_m_product(*ahead)
            hold(pe, xh3_ready, b + 1)
            TR(p_back[0:C, 64:192], xh3[:, :], ident[:, :]).then_inc(xh3_tr, 1)
            if ahead is not None:
                attn0_product(*ahead)
            hold(pe, xh3_t_ready, b + 1)
            M(p_back[:, 192:256], xh3_t[:, :], wqkv_sb[:, 0:C], start=True, stop=True)
            M(p_back[0:C, 256:384], wqkv_sb[:, C:2 * C], xh3_t[:, :], start=True, stop=True)
            M(p_back[0:C, 384:512], wqkv_sb[:, 2 * C:3 * C], xh3_t[:, :], start=True, stop=True
              ).then_inc(qkv_mm, 1)
            hold(pe, ek_t_ready, b + 1)
            TR(p_back[:, 64:128], ek_t[:, :], ident[0:C, 0:C]).then_inc(ek_tr, 1)
            if ahead is not None:
                xh2_transpose(*ahead)
            hold(pe, ek_ready, b + 1)
            M(p_back[0:C, 128:192], ek[:, :], l1_q[:, :], start=True, stop=True).then_inc(l1_a_mm, 1)
            hold(pe, l1_a_ready, b + 1)
            M(p_back[0:C, 256:384], l1_a[:, :], l1_v_t[:, :], start=True, stop=True).then_inc(l1_o_mm, 1)
            hold(pe, l1_x_ready, b + 1)
            for j in range(L1_HEADS):
                last = M(p_back[:, 0:C], l1_x[:, j, :, :].rearrange("d h m -> d (h m)"), wout_sb[:, j, :],
                         start=(j == 0), stop=(j == L1_HEADS - 1))
            last.then_inc(l1_mm, 1)
            if ahead is not None:
                scores(*ahead)
            hold(pe, xn_ready, b + 1)
            TR(p_back[0:C, 64:192], xn[:, :], ident[:, :]).then_inc(xn_tr, 1)
            hold(pe, xn_t_ready, b + 1)
            M(p_back[:, 192:192 + E], xn_t[:, :], wr_sb[:, :], start=True, stop=True).then_inc(logit_mm, 1)
            for e in range(E):
                last = M(p_x[:, HID * e:HID * e + HID], w1_sb[:, e, :], xn_t[:, :], start=True, stop=True)
            last.then_inc(hid_mm, 1)
            hold(pe, hid_ready, b + 1)
            for e in range(E):
                last = M(p_y[:, C * e:C * e + C], hid[:, e, :], w2_sb[:, e, :], start=True, stop=True)
            last.then_inc(y_mm, 1)

        over_batches(pe, tokens, select, back)

    ctx.close()


def kernel(**inputs):
    import numpy as np
    import concourse.bacc as bacc
    from concourse.bass_utils import run_bass_kernel_spmd

    g = {k: np.asarray(v) for k, v in inputs.items()}
    spread = {"conv_w": g["L0_tok_w"], "conv_b": g["L0_tok_b"], "tok_gamma": g["L0_tok_gamma"],
              "tok_beta": g["L0_tok_beta"], "tok_alpha": g["L0_tok_alpha"], "bout": g["L1_attn_bout"],
              "l1_gamma": g["L1_attn_gamma"], "l1_beta": g["L1_attn_beta"], "ffn_gamma": g["L1_ffn_gamma"],
              "ffn_beta": g["L1_ffn_beta"], "br": g["L1_ffn_br"], "b2": g["L1_ffn_b2"]}
    rows = np.concatenate([spread[n].reshape(-1) for n in ROWS])
    arrays = {
        "x": g["x"],
        "rows": np.broadcast_to(rows[None, :], (T, ROW_WORDS)),
        "attn_w": g["L0_attn_W"],
        "wqpk_t": g["L0_ffn_Wq_pk"].reshape(C, GROUPS, DKEY).transpose(2, 1, 0),
        "keys_t": g["L0_ffn_pk_keys"].transpose(3, 0, 2, 1).reshape(DKEY, GROUPS, SUBKEYS),
        "wq": g["L0_ffn_Wq"],
        "table": np.concatenate([g["L0_ffn_keys_table"], g["L0_ffn_values_table"]], axis=1),
        "wo": g["L0_ffn_Wo"].reshape(-1, 128, C).transpose(1, 0, 2),
        "wqkv": g["L1_attn_Wqkv"],
        "wout": np.tile(g["L1_attn_Wout"].reshape(-1, C // L1_HEADS, C).transpose(1, 0, 2), (L1_HEADS, 1, 1)),
        "wr": g["L1_ffn_Wr"],
        "w1": g["L1_ffn_W1"].transpose(1, 0, 2),
        "b1_t": g["L1_ffn_b1"].transpose(1, 0),
        "w2": g["L1_ffn_W2"].transpose(1, 0, 2),
    }
    arrays = {k: np.ascontiguousarray(v) for k, v in arrays.items()}
    nc = bacc.Bacc("TRN2", target_bir_lowering=False, num_devices=1)
    args = [nc.dram_tensor(f"in_{k}", v.shape, F32, kind="ExternalInput").ap() for k, v in arrays.items()]
    out = nc.dram_tensor("out", (B, T, C), F32, kind="ExternalOutput").ap()
    build(nc, *args, out)
    r = run_bass_kernel_spmd(nc, [{f"in_{k}": v for k, v in arrays.items()}], core_ids=[0])
    return r.results[0]["out"]
```

```python
from contextlib import ExitStack

import concourse.bass as bass
from concourse import mybir

F32 = mybir.dt.float32
BF16 = mybir.dt.bfloat16
U32 = mybir.dt.uint32
I32 = mybir.dt.int32
ALU = mybir.AluOpType
ACT = mybir.ActivationFunctionType
AX = mybir.AxisListType

B, T_IN, C = 128, 256, 64
TAPS, STRIDE = 5, 2
T = T_IN // STRIDE
PAD_LOW = ((T - 1) * STRIDE + TAPS - T_IN) // 2
HEADS, SIDES, SUBKEYS, DKEY = 8, 2, 64, 32
GROUPS = SIDES * HEADS
TOPK = 16
KV = 2 * C
E, HID = 8, 128
L1_HEADS = 8
NEG = -3.0e38

GATHERED = HEADS - 1
DENSE = HEADS - 1
CHUNKS = SUBKEYS * SUBKEYS // 128
PER_GROUP = 2
GROUPS_D = CHUNKS // PER_GROUP
EPS_TOK, EPS = 1e-3, 1e-5
Q_SCALE = C ** -0.5

SEGMENTS = []
_off = 0
for _r0, _rows in ((0, 1), (1, 1), (2, 1), (3, 1), (4, 1), (5, 3), (8, 8)):
    _w = TOPK // (_r0 + 1)
    SEGMENTS.append((_r0, _rows, _w, _off))
    _off += _rows * _w
CAND = _off

ROWS = {}
_at = 0
for _name, _n in (("conv_w", TAPS * C), ("conv_b", C), ("tok_gamma", C), ("tok_beta", C), ("tok_alpha", C),
                  ("bout", C), ("l1_gamma", C), ("l1_beta", C), ("ffn_gamma", C), ("ffn_beta", C),
                  ("br", E), ("b2", E * C)):
    ROWS[_name] = (_at, _at + _n)
    _at += _n
ROW_WORDS = _at
N_CONST_DMAS = 13


def build(nc, x, rows, w_mask_src, wqpk_t, keys_t, wq, table, wo, wqkv, wout, wr, w1, b1_t, w2, dense_t, out):
    ctx = ExitStack()

    def sb(name, shape, dt=F32):
        return ctx.enter_context(nc.sbuf_tensor(name, shape, dt))

    def sem(name):
        return ctx.enter_context(nc.semaphore(name))

    def psum(name, shape):
        return ctx.enter_context(nc.psum_tensor(name, shape, F32))

    row = sb("row_consts", [T, ROW_WORDS])
    ident = sb("ident", [128, 128])
    mean_w = sb("mean_w", [128, 128])
    causal = sb("causal", [T, T])
    block8 = sb("block8", [C, C])
    iota_k = sb("iota_k", [T, SUBKEYS])
    iota_cand = iota_k[:, 0:CAND]
    ident_bf = sb("ident_bf", [128, 128], BF16)
    pair_sel = sb("pair_sel", [128, CHUNKS, 128], BF16)
    dense_sb = sb("dense_sb", [128, CHUNKS, KV])
    rank_val = sb("rank_val", [T, SIDES, TOPK], BF16)
    iota_e = sb("iota_e", [T, E])
    table_base = sb("table_base", [T, HEADS])
    attn_w = sb("attn_w", [C, C])
    score_w = sb("score_w", [C, GROUPS * SUBKEYS])
    wq_sb = sb("wq_sb", [C, HEADS * C])
    wo_sb = sb("wo_sb", [128, HEADS * C // 128, C])
    wqkv_sb = sb("wqkv_sb", [C, 3 * C])
    wout_sb = sb("wout_sb", [C, L1_HEADS, C])
    wr_sb = sb("wr_sb", [C, E])
    w1_sb = sb("w1_sb", [C, E, HID])
    b1_sb = sb("b1_sb", [HID, E])
    w2_sb = sb("w2_sb", [HID, E, C])

    def rc(name):
        a, b = ROWS[name]
        return row[:, a:b]

    xwin = [sb(f"xwin{p}", [T, TAPS, C]) for p in range(2)]
    taps = sb("taps", [T, TAPS, C])
    y = sb("y", [T, C])
    stats6 = sb("stats6", [T, 6])
    rowstat = sb("rowstat", [T, 2])
    dev = sb("dev", [T, 1])
    dev_sq = sb("dev_sq", [T, 1])
    tok_mean = sb("tok_mean", [T, 1])
    f_var = sb("f_var", [T, 1])
    f_rstd0 = sb("f_rstd0", [T, 1])
    f_log = sb("f_log", [T, 1])
    f_tmp = sb("f_tmp", [T, 2])
    f_rstd = sb("f_rstd", [T, 1])
    yn, neg_part = taps[:, 0, :], taps[:, 1, :]
    h0 = sb("h0", [T, C])
    xh1 = sb("xh1", [T, C])
    xh1_t = sb("xh1_t", [C, T])
    gram = sb("gram", [C, C])
    attn_m = sb("attn_m", [C, C])
    h1 = [sb(f"h1_{p}", [T, C]) for p in range(2)]
    xh2 = sb("xh2", [T, C])
    xh2_t = [sb(f"xh2_t{p}", [C, T]) for p in range(2)]
    top = sb("top", [T, SIDES, HEADS, TOPK])
    top_i = sb("top_i", [T, SIDES, HEADS, TOPK], U32)
    top_f = sb("top_f", [T, SIDES, HEADS, TOPK])
    sim_rest = sb("sim_rest", [T, GROUPS, SUBKEYS])
    cand = sb("cand", [T, HEADS, CAND])
    cand_rest = sb("cand_rest", [T, HEADS, CAND])
    cand_i = sb("cand_i", [T, HEADS, CAND])
    fin = sb("fin", [T, HEADS, TOPK])
    pos_i = sb("pos_i", [T, HEADS, TOPK], U32)
    pos_f = sb("pos_f", [T, HEADS, TOPK])
    onehot_mem = sb("onehot_mem", [T, TOPK * SUBKEYS])
    onehot = onehot_mem[:, 0:TOPK * CAND].rearrange("t (k c) -> t k c", k=TOPK)
    rank_hot = onehot_mem[:, :].bitcast(BF16).rearrange("t (r s i) -> t r s i", r=TOPK, s=SIDES)
    rest = onehot_mem[:, 0:T]
    cand_last = sb("cand_last", [T, CAND])
    chosen = sb("chosen", [T, CAND])
    below = taps[:, 2:4, :]
    dense_mov = sb("dense_mov", [128, 4, T], BF16)
    dense_inv = [sb(f"dense_inv{p}", [T, 1]) for p in range(2)]
    idx_f = sb("idx_f", [T, HEADS, TOPK])
    idx = [sb(f"idx{p}", [T, HEADS * TOPK], I32) for p in range(2)]
    fin_d = sb("fin_d", [T, HEADS, TOPK])
    fin_e = sb("fin_e", [T, HEADS, TOPK])
    fin_s = sb("fin_s", [T, HEADS])
    fin_r = sb("fin_r", [T, HEADS])
    kv_w = [sb(f"kv_w{p}", [T, HEADS, TOPK]) for p in range(2)]
    gath = [sb(f"gath{p}", [T, GATHERED, TOPK, KV]) for p in range(2)]
    wqpk_sb = gath[1][0:DKEY, 0, 0:8, :].rearrange("d k c -> d (k c)").rearrange("d (g c) -> d g c", g=GROUPS)
    keys_sb = gath[1][0:DKEY, 1, 0:8, :].rearrange("d k c -> d (k c)").rearrange("d (g c) -> d g c", g=GROUPS)
    kv = sb("kv", [T, HEADS, KV])
    prob = sb("prob", [T, HEADS, T])
    q_t = prob[0:C, :, :]
    attn_mem = sb("attn_mem", [T, 2 * HEADS * C])
    k_t = attn_mem[0:C, :].rearrange("d (h t) -> d h t", h=HEADS)
    neg_max = sb("neg_max", [T, HEADS])
    row_sum = sb("row_sum", [T, HEADS])
    row_inv = sb("row_inv", [T, HEADS])
    prob_t = sim_rest[:, :, :].rearrange("t g k -> t (g k)").rearrange("t (h i) -> t h i", h=HEADS)
    attn_o = attn_mem[:, 0:HEADS * C]
    attn_o_t = attn_mem[:, HEADS * C:].rearrange("d (c t) -> d c t", t=T)
    dense_e = [sim_rest[:, 4 * g:4 * g + 4, :].rearrange("p a b -> p (a b)").rearrange("p (l t) -> p l t", t=T)
               for g in range(2)]
    dense_w = [sim_rest[:, 4 * g + 8:4 * g + 12, :].rearrange("p a b -> p (a b)").rearrange("p (l t) -> p l t", t=T)
               for g in range(2)]
    b_stats6 = sb("b_stats6", [T, 6])
    b_mv = sb("b_mv", [T, 2])
    b_var = sb("b_var", [T, 1])
    b_rstd0 = sb("b_rstd0", [T, 1])
    b_log = sb("b_log", [T, 1])
    b_tmp = sb("b_tmp", [T, 2])
    b_rstd = sb("b_rstd", [T, 1])
    h2 = sb("h2", [T, C])
    xh3 = sb("xh3", [T, C])
    xh3_t = sb("xh3_t", [C, T])
    l1_q = sb("l1_q", [T, C])
    l1_v_t = sb("l1_v_t", [C, T])
    neg_kmax = sb("neg_kmax", [C, 1])
    ek_t = sb("ek_t", [C, T])
    k_sum = sb("k_sum", [C, 1])
    k_inv = sb("k_inv", [C, 1])
    ek = sb("ek", [T, C])
    l1_a = sb("l1_a", [C, C])
    l1_x = prob[0:C, :, :].rearrange("d h t -> d (h t)").rearrange("d (j h m) -> d j h m", j=L1_HEADS, h=L1_HEADS)
    z = sb("z", [T, C])
    h3 = sb("h3", [T, C])
    xn = sb("xn", [T, C])
    xn_t = sb("xn_t", [C, T])
    logit = sb("logit", [T, E])
    best = sb("best", [T, 8])
    best_i = sb("best_i", [T, 8], U32)
    best_f = sb("best_f", [T, 2])
    gap = sb("gap", [T, 1])
    gap_e = sb("gap_e", [T, 1])
    gap_d = sb("gap_d", [T, 1])
    mix = sb("mix", [T, 2])
    pick = sb("pick", [T, 2, E])
    w_full = sb("w_full", [T, E])
    hid = prob
    y_e = attn_o.rearrange("t (e c) -> t e c", e=E)
    y_sum = sb("y_sum", [T, C])
    h_out = [sb(f"h_out{p}", [T, C]) for p in range(2)]

    p_front = psum("p_front", [128, 512])
    p_sim = psum("p_sim", [128, 1024])
    p_back = psum("p_back", [128, 512])
    p_x = psum("p_x", [128, 1024])
    p_y = psum("p_y", [128, 1024])

    consts_loaded = sem("consts_loaded")
    pool_consts = sem("pool_consts")
    pool_ones = sem("pool_ones")
    score_mm = sem("score_mm")
    score_ready = sem("score_ready")
    x_loaded = [sem(f"x_loaded{p}") for p in range(2)]
    conv_done = sem("conv_done")
    f_var_ready = sem("f_var_ready")
    f_rstd_ready = sem("f_rstd_ready")
    rowstats_ready = sem("rowstats_ready")
    mean_ready = sem("mean_ready")
    dev_ready = sem("dev_ready")
    var_ready = sem("var_ready")
    xh1_ready = sem("xh1_ready")
    gram_mm = sem("gram_mm")
    gram_ready = sem("gram_ready")
    attn_m_mm = sem("attn_m_mm")
    attn_m_ready = sem("attn_m_ready")
    attn0_mm = sem("attn0_mm")
    xh2_ready = sem("xh2_ready")
    xh2_tr = sem("xh2_tr")
    xh2_t_ready = sem("xh2_t_ready")
    sim_mm = sem("sim_mm")
    idx_ready = sem("idx_ready")
    fin_d_ready = sem("fin_d_ready")
    fin_e_ready = sem("fin_e_ready")
    kv_w_ready = sem("kv_w_ready")
    gathered = [[sem(f"gathered{p}_{h}") for h in range(GATHERED)] for p in range(2)]
    scaled = sem("scaled")
    kv_mm = sem("kv_mm")
    kv_ready = sem("kv_ready")
    ranks_ready = sem("ranks_ready")
    ranks_tr = sem("ranks_tr")
    dense_mov_ready = sem("dense_mov_ready")
    pair_mm = sem("pair_mm")
    dense_e_ready = sem("dense_e_ready")
    dense_w_ready = sem("dense_w_ready")
    q_mm = sem("q_mm")
    q_ready = sem("q_ready")
    k_tr = sem("k_tr")
    k_t_ready = sem("k_t_ready")
    s_mm = sem("s_mm")
    neg_max_ready = sem("neg_max_ready")
    prob_ready = sem("prob_ready")
    prob_tr = sem("prob_tr")
    prob_t_ready = sem("prob_t_ready")
    attn_mm = sem("attn_mm")
    attn_o_ready = sem("attn_o_ready")
    attn_o_tr = sem("attn_o_tr")
    attn_o_t_ready = sem("attn_o_t_ready")
    wo_mm = sem("wo_mm")
    b_var_ready = sem("b_var_ready")
    b_rstd_ready = sem("b_rstd_ready")
    xh3_ready = sem("xh3_ready")
    xh3_tr = sem("xh3_tr")
    xh3_t_ready = sem("xh3_t_ready")
    qkv_mm = sem("qkv_mm")
    neg_kmax_ready = sem("neg_kmax_ready")
    ek_t_ready = sem("ek_t_ready")
    ek_tr = sem("ek_tr")
    ek_ready = sem("ek_ready")
    l1_a_mm = sem("l1_a_mm")
    l1_a_ready = sem("l1_a_ready")
    l1_o_mm = sem("l1_o_mm")
    l1_x_ready = sem("l1_x_ready")
    l1_mm = sem("l1_mm")
    xn_ready = sem("xn_ready")
    xn_tr = sem("xn_tr")
    xn_t_ready = sem("xn_t_ready")
    logit_mm = sem("logit_mm")
    gap_ready = sem("gap_ready")
    gap_e_ready = sem("gap_e_ready")
    hid_mm = sem("hid_mm")
    hid_ready = sem("hid_ready")
    y_mm = sem("y_mm")
    sums_free = sem("sums_free")
    out_ready = sem("out_ready")
    out_free = [sem(f"out_free{p}") for p in range(2)]

    waits_passed = sem("waits_passed")

    BUILT = 7
    POOL_CONSTS = 12

    def hold(eng, s, value):
        eng.wait_ge(s, value)
        eng.sem_inc(waits_passed, 1)

    DECODED = 3
    EARLY = 6
    FIRST = 2

    def at_sum(h):
        slot = h if h == DENSE else h + 4 if h < 3 else h - 3
        return slice(KV * slot, KV * slot + KV)

    def over_batches(eng, tokens, subkeys, select, dense_start, dense, back):
        tokens(0, 0)
        subkeys(0, 0)
        select(0, 0, None)
        dense_start(0, 0)
        dense(0, 0, 0, GROUPS_D)
        tokens(0, 1)
        subkeys(0, 1)
        select(0, 1, (0, 0))
        with eng.Fori(0, B // 2 - 1) as it:
            for p in range(2):
                back(it, p, (it + (p + 1) // 2, 1 - p), (it + 1, p))
                select(it + 1, p, (it + (p + 1) // 2, 1 - p))
        back(B // 2 - 1, 0, (B // 2 - 1, 1), None)
        back(B // 2 - 1, 1, None, None)

    block = ctx.enter_context(nc.Block())

    @block.sync
    def _(sp):
        for dst, src in ((row[:, :], rows), (attn_w[:, :], w_mask_src), (wqpk_sb[:, :, :], wqpk_t),
                         (keys_sb[:, :, :], keys_t), (wq_sb[:, :], wq), (wo_sb[:, :, :], wo),
                         (wqkv_sb[:, :], wqkv), (wout_sb[:, :, :], wout), (wr_sb[:, :], wr), (dense_sb[:, :, :], dense_t)):
            sp.dma_start(dst, src).then_inc(consts_loaded, 16)

        def load_window(it, p):
            b = 2 * it + p
            xb = x[b] if isinstance(b, int) else x[bass.ds(b, 1)].rearrange("o t c -> (o t) c")
            w = xwin[p]
            sp.dma_start(w[:, 1:3, :], xb.rearrange("(t k) c -> t k c", k=2)).then_inc(x_loaded[p], 16)
            sp.dma_start(w[1:T, 0, :], xb.rearrange("(t k) c -> t k c", k=2)[0:T - 1, 1, :]
                         ).then_inc(x_loaded[p], 16)
            sp.dma_start(w[0:T - 1, 3:5, :], xb.rearrange("(t k) c -> t k c", k=2)[1:T, :, :]
                         ).then_inc(x_loaded[p], 16)

        def store(it, p):
            b = 2 * it + p
            ob = out[b] if isinstance(b, int) else out[bass.ds(b, 1)].rearrange("o t c -> (o t) c")
            sp.wait_ge(out_ready, b + 1)
            sp.dma_start(ob, h_out[p][:, :]).then_inc(out_free[p], 16)

        sp.sem_inc(out_free[0], 16)
        sp.sem_inc(out_free[1], 16)
        sp.wait_ge(pool_ones, BUILT)
        load_window(0, 0)
        load_window(0, 1)
        for p in range(2):
            sp.wait_ge(conv_done, p + 1)
            load_window(1, p)
        with sp.Fori(0, B // 2 - 2) as it:
            for p in range(2):
                sp.wait_ge(conv_done, 2 * it + p + 3)
                load_window(it + 2, p)
                store(it, p)
        for it in (B // 2 - 2, B // 2 - 1):
            for p in range(2):
                store(it, p)
        for p in range(2):
            sp.wait_ge(out_free[p], 16 * (B // 2 + 1))

    @block.gpsimd
    def _(pool):
        nc.gpsimd.memset(ident[:, :], 0.0).then_inc(pool_ones, 1)
        nc.gpsimd.memset(causal[:, :], 0.0).then_inc(pool_ones, 1)
        nc.gpsimd.memset(block8[:, :], 1.0).then_inc(pool_ones, 1)
        nc.gpsimd.memset(mean_w[:, :], 1.0 / 128).then_inc(pool_ones, 1)
        for p in range(2):
            nc.gpsimd.memset(xwin[p][:, :, :].rearrange("t k c -> t (k c)"), 0.0).then_inc(pool_ones, 1)
        nc.gpsimd.memset(pair_sel[:, :, :].rearrange("k c m -> k (c m)"), 1.0).then_inc(pool_ones, 1)
        pool.wait_ge(pool_ones, BUILT)
        nc.gpsimd.affine_select(out=ident[:, :], in_=ident[:, :], pattern=[[-1, 128]], compare_op=ALU.not_equal,
                                fill=1.0, base=0, channel_multiplier=1).then_inc(pool_consts, 1)
        nc.gpsimd.affine_select(out=causal[:, :], in_=causal[:, :], pattern=[[-1, T]], compare_op=ALU.is_ge,
                                fill=NEG, base=0, channel_multiplier=1).then_inc(pool_consts, 1)
        b8 = block8[:, :].rearrange("r (g j) -> r g j", g=L1_HEADS)
        nc.gpsimd.affine_select(out=b8, in_=b8, pattern=[[-8, L1_HEADS], [0, 8]], compare_op=ALU.is_ge,
                                fill=0.0, base=0, channel_multiplier=1).then_inc(pool_consts, 1)
        pool.wait_ge(pool_consts, 3)
        nc.gpsimd.affine_select(out=b8, in_=b8, pattern=[[8, L1_HEADS], [0, 8]], compare_op=ALU.is_ge,
                                fill=0.0, base=7, channel_multiplier=-1).then_inc(pool_consts, 1)
        nc.gpsimd.iota(iota_k[:, :], pattern=[[1, SUBKEYS]], base=0, channel_multiplier=0,
                       allow_small_or_imprecise_dtypes=True).then_inc(pool_consts, 1)
        nc.gpsimd.iota(iota_e[:, :], pattern=[[1, E]], base=0, channel_multiplier=0,
                       allow_small_or_imprecise_dtypes=True).then_inc(pool_consts, 1)
        nc.gpsimd.iota(table_base[:, :], pattern=[[SUBKEYS * SUBKEYS, HEADS]], base=0, channel_multiplier=0,
                       allow_small_or_imprecise_dtypes=True).then_inc(pool_consts, 1)
        nc.gpsimd.iota(rank_val[:, 1, :], pattern=[[-1, TOPK]], base=SUBKEYS, channel_multiplier=0,
                       allow_small_or_imprecise_dtypes=True).then_inc(pool_consts, 1)
        nc.gpsimd.tensor_copy(ident_bf[:, :], ident[:, :]).then_inc(pool_consts, 1)
        top_half = pair_sel[0:SUBKEYS, :, :].rearrange("k c (l i) -> k (c l) i", l=2)
        pool.wait_ge(pool_consts, 9)
        nc.gpsimd.affine_select(out=top_half, in_=top_half, pattern=[[0, 2 * CHUNKS], [-1, SUBKEYS]],
                                compare_op=ALU.is_equal, fill=0.0, base=0, channel_multiplier=1
                                ).then_inc(pool_consts, 1)
        low_half = pair_sel[SUBKEYS:128, :, :].rearrange("k c (l i) -> k (c l) i", l=2)
        pool.wait_ge(pool_consts, 10)
        nc.gpsimd.affine_select(out=low_half, in_=low_half, pattern=[[-1, 2 * CHUNKS], [0, SUBKEYS]],
                                compare_op=ALU.is_equal, fill=0.0, base=0, channel_multiplier=1
                                ).then_inc(pool_consts, 1)
        pool.wait_ge(consts_loaded, 16 * N_CONST_DMAS)
        nc.gpsimd.affine_select(out=attn_w[:, :], in_=attn_w[:, :], pattern=[[1, C]], compare_op=ALU.is_gt,
                                fill=0.0, base=0, channel_multiplier=-1).then_inc(pool_consts, 1)

        def gather(it, p):
            for h in range(GATHERED):
                hold(pool, idx_ready, GATHERED * (2 * it + p) + h + 1)
                for k in range(TOPK):
                    c = h * TOPK + k
                    nc.gpsimd.indirect_dma_start(
                        out=gath[p][:, h, k, :], out_offset=None, in_=table[:, :],
                        in_offset=bass.IndirectOffsetOnAxis(ap=idx[p][:, c:c + 1], axis=0),
                    ).then_inc(gathered[p][h], 16)

        with pool.Fori(0, B // 2) as it:
            for p in range(2):
                gather(it, p)

    @block.vector
    def _(dve):
        V = nc.vector
        V_sync = dve.drain

        def normalise(dst, src, mean, rstd):
            return V.tensor_scalar(dst, src, mean, rstd, ALU.subtract, ALU.mult)

        def newton(var, r0, tmp, dst):
            V.scalar_tensor_tensor(tmp[:, 0:1], r0[:, :], r0[:, 0:1], var[:, :], ALU.mult, ALU.mult)
            V_sync()
            V.tensor_scalar(tmp[:, 1:2], tmp[:, 0:1], -0.5, 1.5, ALU.mult, ALU.add)
            V_sync()
            V.tensor_tensor(dst[:, :], r0[:, :], tmp[:, 1:2], ALU.mult)
            V_sync()

        def front_var(src):
            V.bn_stats(stats6[:, :], src)
            V_sync()
            V.bn_aggr(rowstat[:, :], stats6[:, :])
            V_sync()
            V.tensor_scalar(f_var[:, :], rowstat[:, 1:2], EPS, None, ALU.add).then_inc(f_var_ready, 1)

        def front_norm(dst, src, count, ready):
            dve.wait_ge(f_rstd_ready, count)
            newton(f_var, f_rstd0, f_tmp, f_rstd)
            normalise(dst, src, rowstat[:, 0:1], f_rstd[:, 0:1]).then_inc(ready, 1)
            V_sync()

        def back_var(src):
            V.bn_stats(b_stats6[:, :], src)
            V_sync()
            V.bn_aggr(b_mv[:, :], b_stats6[:, :])
            V_sync()
            V.tensor_scalar(b_var[:, :], b_mv[:, 1:2], EPS, None, ALU.add).then_inc(b_var_ready, 1)

        def back_norm(dst, src, count):
            dve.wait_ge(b_rstd_ready, count)
            newton(b_var, b_rstd0, b_tmp, b_rstd)
            last = normalise(dst, src, b_mv[:, 0:1], b_rstd[:, 0:1])
            V_sync()
            return last

        def back_scale(x, which, count):
            V.scalar_tensor_tensor(x, x, b_mv[:, 0:1], rc(which + "_gamma"), ALU.subtract, ALU.mult)
            dve.wait_ge(b_rstd_ready, count)
            newton(b_var, b_rstd0, b_tmp, b_rstd)
            return V.scalar_tensor_tensor(x, x, b_rstd[:, 0:1], rc(which + "_beta"), ALU.mult, ALU.add)

        def conv(it, p):
            dve.wait_ge(x_loaded[p], 48 * it + 48)
            V.tensor_tensor(taps[:, :, :], xwin[p][:, :, :],
                            rc("conv_w").rearrange("t (k c) -> t k c", k=TAPS), ALU.mult).then_inc(conv_done, 1)
            V_sync()
            V.tensor_reduce(y[:, :], taps[:, :, :].rearrange("t k c -> t c k"), AX.X, ALU.add)
            V_sync()
            V.tensor_tensor(y[:, :], y[:, :], rc("conv_b"), ALU.add)
            V_sync()
            V.bn_stats(stats6[:, :], y[:, :])
            V_sync()
            V.bn_aggr(rowstat[:, :], stats6[:, :]).then_inc(rowstats_ready, 1)

        def deviation(it, p):
            V_sync()
            dve.wait_ge(mean_ready, 2 * it + p + 1)
            V.tensor_copy(tok_mean[:, :], p_front[:, 0:1])
            V_sync()
            V.tensor_tensor(dev[:, :], rowstat[:, 0:1], tok_mean[:, :], ALU.subtract)
            V_sync()
            V.scalar_tensor_tensor(dev_sq[:, :], dev[:, :], dev[:, 0:1], rowstat[:, 1:2], ALU.mult,
                                   ALU.add).then_inc(dev_ready, 1)

        def variance(it, p):
            dve.wait_ge(var_ready, 2 * it + p + 1)
            V.tensor_scalar(f_var[:, :], p_front[:, 1:2], EPS_TOK, None, ALU.add).then_inc(f_var_ready, 1)

        def prelu(it, p):
            b = 2 * it + p
            V.scalar_tensor_tensor(yn, y[:, :], tok_mean[:, 0:1], rc("tok_gamma"), ALU.subtract, ALU.mult)
            dve.wait_ge(f_rstd_ready, 3 * b + 1)
            newton(f_var, f_rstd0, f_tmp, f_rstd)
            V.scalar_tensor_tensor(yn, yn, f_rstd[:, 0:1], rc("tok_beta"), ALU.mult, ALU.add)
            V_sync()
            V.scalar_tensor_tensor(neg_part, yn, 0.0, rc("tok_alpha"), ALU.min, ALU.mult)
            V_sync()
            V.scalar_tensor_tensor(h0[:, :], yn, 0.0, neg_part, ALU.max, ALU.add)
            V_sync()
            front_var(h0[:, :])

        def norm1(it, p):
            front_norm(xh1[:, :], h0[:, :], 3 * (2 * it + p) + 2, xh1_ready)

        def add_attn0(it, p):
            dve.wait_ge(attn0_mm, 2 * it + p + 1)
            V.tensor_tensor(h1[p][:, :], h0[:, :], p_front[:, 384:448], ALU.add)
            V_sync()
            front_var(h1[p][:, :])

        def norm2(it, p):
            front_norm(xh2[:, :], h1[p][:, :], 3 * (2 * it + p) + 3, xh2_ready)

        def tokens(it, p):
            for step in (conv, deviation, variance, prelu, norm1, add_attn0, norm2):
                step(it, p)

        def subkeys(it, p):
            hold(dve, sim_mm, 2 * it + p + 1)
            sim = p_sim[:, :].rearrange("t (g k) -> t g k", g=GROUPS)
            tops = top[:, :, :, :].rearrange("t s h k -> t (s h) k")
            tops_i = top_i[:, :, :, :].rearrange("t s h k -> t (s h) k")
            for g in range(GROUPS):
                V.max(tops[:, g, 0:8], sim[:, g, :])
            V_sync()
            for g in range(GROUPS):
                V.max_index(tops_i[:, g, 0:8], tops[:, g, 0:8], sim[:, g, :])
                V.match_replace(sim_rest[:, g, :], tops[:, g, 0:8], sim[:, g, :], NEG)
            V_sync()
            for g in range(GROUPS):
                V.max(tops[:, g, 8:16], sim_rest[:, g, :])
            V_sync()
            for g in range(GROUPS):
                V.max_index(tops_i[:, g, 8:16], tops[:, g, 8:16], sim_rest[:, g, :])
            V_sync()

        def decode(it, p, first, end):
            for h in range(first, end):
                V.tensor_tensor(onehot, iota_cand[:, None, :].to_broadcast([T, TOPK, CAND]),
                                pos_f[:, h, :, None].to_broadcast([T, TOPK, CAND]), ALU.is_equal)
                V_sync()
                V.tensor_tensor(onehot, onehot, cand_i[:, h, None, :].to_broadcast([T, TOPK, CAND]), ALU.mult)
                V_sync()
                V.tensor_reduce(idx_f[:, h, :], onehot, AX.X, ALU.add)
                V_sync()
                V.tensor_copy(idx[p][:, TOPK * h:TOPK * h + TOPK], idx_f[:, h, :]).then_inc(idx_ready, 1)

        def select(it, p, before):
            b = 2 * it + p
            V.tensor_tensor(top_f[:, 0], top_i[:, 0], table_base[:, :, None].to_broadcast([T, HEADS, TOPK]),
                            ALU.add)
            V.tensor_scalar(top_f[:, 1], top_i[:, 1], float(SUBKEYS), None, ALU.mult)
            V_sync()
            for src, dst in ((top, cand), (top_f, cand_i)):
                for r0, n, w, off in SEGMENTS:
                    o = dst[:, :, off:off + n * w].rearrange("t h (r c) -> t h r c", r=n)
                    a = src[:, 0, :, r0:r0 + n, None].to_broadcast([T, HEADS, n, w])
                    c = src[:, 1, :, None, 0:w].to_broadcast([T, HEADS, n, w])
                    V.tensor_tensor(o, a, c, ALU.add)
            V_sync()
            for h in range(HEADS):
                V.max(fin[:, h, 0:8], cand[:, h, :])
            V_sync()
            for h in range(HEADS):
                V.max_index(pos_i[:, h, 0:8], fin[:, h, 0:8], cand[:, h, :])
                V.match_replace(cand_rest[:, h, :], fin[:, h, 0:8], cand[:, h, :], NEG)
            V_sync()
            for h in range(HEADS):
                V.max(fin[:, h, 8:16], cand_rest[:, h, :])
            V_sync()
            for h in range(HEADS):
                V.max_index(pos_i[:, h, 8:16], fin[:, h, 8:16], cand_rest[:, h, :])
            V_sync()
            V.tensor_copy(pos_f[:, :, :], pos_i[:, :, :])
            V.tensor_tensor(fin_d[:, :, :], fin[:, :, :], fin[:, :, 0:1].to_broadcast([T, HEADS, TOPK]),
                            ALU.subtract).then_inc(fin_d_ready, 1)
            V_sync()
            decode(it, p, 0, GATHERED if before is None else DECODED)
            V.match_replace(cand_last[:, :], fin[:, DENSE, 8:16], cand_rest[:, DENSE, :], NEG)
            V.tensor_tensor(below, p_sim[:, :].rearrange("t (s h k) -> t s h k", s=SIDES, h=HEADS)[:, :, DENSE, :],
                            top[:, :, DENSE, 0:1].to_broadcast([T, SIDES, SUBKEYS]), ALU.subtract)
            V.tensor_tensor(rank_hot, iota_k[:, None, None, :].to_broadcast([T, TOPK, SIDES, SUBKEYS]),
                            top_i[:, :, DENSE, :].rearrange("t s r -> t r s")[:, :, :, None]
                            .to_broadcast([T, TOPK, SIDES, SUBKEYS]), ALU.is_equal)
            V_sync()
            V.tensor_scalar(chosen[:, :], cand_last[:, :], NEG, None, ALU.is_equal)
            V_sync()
            with nc.allow_low_precision(reason="counts of 16 at most"):
                for r0, n, w, off in SEGMENTS:
                    V.tensor_reduce(rank_val[:, 0, r0:r0 + n],
                                    chosen[:, off:off + n * w].rearrange("t (r c) -> t r c", r=n), AX.X, ALU.add)
            V_sync()
            V.tensor_tensor(rank_hot, rank_hot,
                            rank_val[:, :, :].rearrange("t s r -> t r s")[:, :, :, None]
                            .to_broadcast([T, TOPK, SIDES, SUBKEYS]), ALU.mult).then_inc(ranks_ready, 1)
            dve.wait_ge(fin_e_ready, b + 1)
            V.tensor_reduce(fin_s[:, :], fin_e[:, :, :], AX.X, ALU.add)
            V_sync()
            V.reciprocal(fin_r[:, :], fin_s[:, :])
            V_sync()
            V.tensor_copy(dense_inv[p][:, :], fin_r[:, DENSE:DENSE + 1])
            V.tensor_tensor(kv_w[p][:, :, :], fin_e[:, :, :],
                            fin_r[:, :, None].to_broadcast([T, HEADS, TOPK]), ALU.mult).then_inc(kv_w_ready, 1)
            V_sync()

        def dense_start(it, p):
            dve.wait_ge(ranks_tr, 2 * it + p + 1)
            V.tensor_copy(dense_mov[:, 0, :], p_back[:, 128:256])
            V.tensor_copy(dense_mov[:, 1, :], p_back[:, 0:128])
            V_sync()
            V.tensor_tensor(rest, p_back[:, 0:128], dense_mov[:, 1, :], ALU.subtract)
            V_sync()
            V.tensor_copy(dense_mov[:, 2, :], rest)
            V_sync()
            V.tensor_tensor(dense_mov[:, 3, :], rest, dense_mov[:, 2, :], ALU.subtract).then_inc(dense_mov_ready, 1)

        def dense(it, p, first, end):
            for g in range(first, end):
                dve.wait_ge(dense_e_ready, GROUPS_D * (2 * it + p) + g + 1)
                V.scalar_tensor_tensor(
                    dense_w[g % 2],
                    p_sim[:, 512 * (g % 2):512 * (g % 2) + 512].rearrange("p (l d t) -> p l d t", d=2, t=T)[:, :, 0, :],
                    float(SUBKEYS), dense_e[g % 2], ALU.is_gt, ALU.mult).then_inc(dense_w_ready, 1)

        def back(it, p, following, ahead):
            b = 2 * it + p
            if following is not None:
                dense_start(*following)
            if ahead is not None:
                conv(*ahead)
                deviation(*ahead)
                variance(*ahead)
            dve.wait_ge(s_mm, b + 1)
            V.tensor_tensor(prob[:, :, :], p_y[:, :].rearrange("t (h j) -> t h j", h=HEADS),
                            causal[:, None, :].to_broadcast([T, HEADS, T]), ALU.add)
            V_sync()
            V.tensor_reduce(neg_max[:, :], prob[:, :, :], AX.X, ALU.max, negate=True).then_inc(neg_max_ready, 1)
            if following is not None:
                decode(*following, DECODED, DECODED + 1)
            dve.wait_ge(prob_ready, b + 1)
            V.reciprocal(row_inv[:, :], row_sum[:, :])
            V_sync()
            if ahead is not None:
                prelu(*ahead)
            if following is not None:
                decode(*following, DECODED + 1, DECODED + 2)
            dve.wait_ge(attn_mm, b + 1)
            V.tensor_tensor(attn_o.rearrange("t (h d) -> t h d", h=HEADS),
                            p_y[:, 0:512].rearrange("t (h d) -> t h d", h=HEADS),
                            row_inv[:, :, None].to_broadcast([T, HEADS, C]), ALU.mult).then_inc(attn_o_ready, 1)
            if ahead is not None:
                norm1(*ahead)
            dve.wait_ge(wo_mm, b + 1)
            V.tensor_tensor(h2[:, :], h1[p][:, :], p_back[:, 0:C], ALU.add)
            V_sync()
            back_var(h2[:, :])
            if following is not None:
                dense(*following, 0, 2)
            back_norm(xh3[:, :], h2[:, :], 4 * b + 1)
            dve.sem_inc(xh3_ready, 1)
            if ahead is not None:
                add_attn0(*ahead)
            if following is not None:
                dense(*following, 2, 4)
            if following is not None:
                decode(*following, DECODED + 2, DECODED + 3)
            dve.wait_ge(qkv_mm, b + 1)
            V.tensor_reduce(neg_kmax[:, :], p_back[0:C, 256:384], AX.X, ALU.max, negate=True
                            ).then_inc(neg_kmax_ready, 1)
            if ahead is not None:
                norm2(*ahead)
            if following is not None:
                dense(*following, 4, 6)
            dve.wait_ge(ek_t_ready, b + 1)
            V.reciprocal(k_inv[:, :], k_sum[:, :])
            V_sync()
            dve.wait_ge(l1_a_mm, b + 1)
            V.scalar_tensor_tensor(l1_a[:, :], p_back[0:C, 128:192], k_inv[:, 0:1], block8[:, :], ALU.mult,
                                   ALU.mult).then_inc(l1_a_ready, 1)
            if following is not None:
                dense(*following, 6, 8)
            dve.wait_ge(l1_o_mm, b + 1)
            V.tensor_tensor(l1_x[:, :, :, :],
                            p_back[0:C, 256:384].rearrange("d (m j) -> d j m", j=L1_HEADS)[:, :, None, :]
                            .to_broadcast([C, L1_HEADS, L1_HEADS, T // L1_HEADS]),
                            block8[:, :].rearrange("d (h e) -> d h e", e=C // L1_HEADS)[:, None, :, 0:1]
                            .to_broadcast([C, L1_HEADS, L1_HEADS, T // L1_HEADS]), ALU.mult
                            ).then_inc(l1_x_ready, 1)
            if following is not None:
                decode(*following, DECODED + 3, DECODED + 4)
            dve.wait_ge(l1_mm, b + 1)
            V.tensor_tensor(z[:, :], p_back[:, 0:C], rc("bout"), ALU.add)
            V_sync()
            back_var(z[:, :])
            if following is not None:
                dense(*following, 8, 12)
            back_scale(z[:, :], "l1", 4 * b + 2)
            V_sync()
            V.tensor_tensor(h3[:, :], h2[:, :], z[:, :], ALU.add)
            V_sync()
            back_var(h3[:, :])
            if following is not None:
                dense(*following, 12, 14)
            back_norm(xn[:, :], h3[:, :], 4 * b + 3)
            back_var(xn[:, :])
            if following is not None:
                dense(*following, 14, 16)
            back_scale(xn[:, :], "ffn", 4 * b + 4).then_inc(xn_ready, 1)
            dve.wait_ge(logit_mm, b + 1)
            V.tensor_tensor(logit[:, :], p_back[:, 192:192 + E], rc("br"), ALU.add)
            V_sync()
            V.max(best[:, :], logit[:, :])
            V_sync()
            V.max_index(best_i[:, :], best[:, :], logit[:, :])
            V.tensor_tensor(gap[:, :], best[:, 1:2], best[:, 0:1], ALU.subtract).then_inc(gap_ready, 1)
            V_sync()
            V.tensor_copy(best_f[:, :], best_i[:, 0:2])
            V_sync()
            dve.wait_ge(gap_e_ready, b + 1)
            V.tensor_scalar(gap_d[:, :], gap_e[:, :], 1.0, None, ALU.add)
            V_sync()
            V.reciprocal(mix[:, 0:1], gap_d[:, :])
            V_sync()
            V.tensor_tensor(mix[:, 1:2], mix[:, 0:1], gap_e[:, :], ALU.mult)
            V_sync()
            for j in range(2):
                V.tensor_scalar(pick[:, j, :], iota_e[:, :], best_f[:, j:j + 1], mix[:, j:j + 1],
                                ALU.is_equal, ALU.mult)
            V_sync()
            V.tensor_tensor(w_full[:, :], pick[:, 0, :], pick[:, 1, :], ALU.add)
            V_sync()
            if ahead is not None:
                subkeys(*ahead)
            dve.wait_ge(y_mm, b + 1)
            V.tensor_tensor(y_e[:, :, :], p_y[:, 0:512].rearrange("t (e c) -> t e c", e=E),
                            rc("b2").rearrange("t (e c) -> t e c", e=E), ALU.add).then_inc(sums_free, 1)
            V_sync()
            V.tensor_tensor(y_e[:, :, :], y_e[:, :, :], w_full[:, :, None].to_broadcast([T, E, C]), ALU.mult)
            V_sync()
            V.tensor_reduce(y_sum[:, :], y_e[:, :, :].rearrange("t e c -> t c e"), AX.X, ALU.add)
            V_sync()
            dve.wait_ge(out_free[p], 16 * it + 16)
            V.tensor_tensor(h_out[p][:, :], h3[:, :], y_sum[:, :], ALU.add).then_inc(out_ready, 1)
            V_sync()

        dve.sem_inc(sums_free, 1)
        dve.wait_ge(consts_loaded, 16 * N_CONST_DMAS)
        dve.wait_ge(pool_consts, POOL_CONSTS)
        over_batches(dve, tokens, subkeys, select, dense_start, dense, back)

    @block.scalar
    def _(act):
        A = nc.scalar
        act.dma_start(w1_sb[:, :, :], w1).then_inc(consts_loaded, 16)
        act.dma_start(w2_sb[:, :, :], w2).then_inc(consts_loaded, 16)
        act.dma_start(b1_sb[:, :], b1_t).then_inc(consts_loaded, 16)
        A.preload_act_table_set("natural_log_exp_and_others")
        act.wait_ge(score_mm, 1)
        for c in range(2):
            last = A.copy(score_w[:, 512 * c:512 * c + 512], p_sim[0:C, 512 * c:512 * c + 512])
        last.then_inc(score_ready, 1)

        def root(var_sem, rstd_sem, count, var, log, rstd0):
            act.wait_ge(var_sem, count)
            A.activation(log[:, :], var[:, :], ACT.Ln)
            act.drain()
            A.activation(rstd0[:, :], log[:, :], ACT.Exp, scale=-0.5).then_inc(rstd_sem, 1)

        def queries(it, p):
            act.wait_ge(q_mm, 2 * it + p + 1)
            for c in range(2):
                last = A.activation(q_t[:, 4 * c:4 * c + 4, :].rearrange("d h t -> d (h t)"),
                                    p_x[0:C, 512 * c:512 * c + 512], ACT.Copy, scale=Q_SCALE)
            last.then_inc(q_ready, 1)

        def weigh(it, p, first, end):
            act.wait_ge(kv_w_ready, 2 * it + p + 1)
            half = TOPK // 2
            for at in range(int(2 * first), int(2 * end)):
                h = at // 2
                if at % 2 == 0:
                    act.wait_ge(gathered[p][h], 16 * TOPK * it + 16 * TOPK)
                for k in range(at % 2 * half, at % 2 * half + half):
                    last = A.activation(gath[p][:, h, k, :], gath[p][:, h, k, :], ACT.Copy,
                                        scale=kv_w[p][:, h, k:k + 1])
                if at % 2 == 1:
                    last.then_inc(scaled, 1)

        def front_root(it, p, nth):
            root(f_var_ready, f_rstd_ready, 3 * (2 * it + p) + nth, f_var, f_log, f_rstd0)

        def gram_copies(it, p):
            act.wait_ge(gram_mm, 2 * it + p + 1)
            A.copy(gram[:, :], p_front[0:C, 256:320])
            A.copy(xh1_t[:, :], p_front[0:C, 128:256]).then_inc(gram_ready, 1)

        def attn_m_copy(it, p):
            act.wait_ge(attn_m_mm, 2 * it + p + 1)
            A.copy(attn_m[:, :], p_front[0:C, 320:384]).then_inc(attn_m_ready, 1)

        def xh2_copy(it, p):
            act.wait_ge(xh2_tr, 2 * it + p + 1)
            A.copy(xh2_t[p][:, :], p_front[0:C, 128:256]).then_inc(xh2_t_ready, 1)

        def tokens(it, p):
            front_root(it, p, 1)
            front_root(it, p, 2)
            gram_copies(it, p)
            attn_m_copy(it, p)
            front_root(it, p, 3)
            xh2_copy(it, p)

        def subkeys(it, p):
            pass

        def select(it, p, before):
            if before is not None:
                weigh(*before, 0 if isinstance(it, int) else FIRST, FIRST + 1)
                queries(*before)
                weigh(*before, FIRST + 1, EARLY)
            act.wait_ge(fin_d_ready, 2 * it + p + 1)
            A.activation(fin_e[:, :, :], fin_d[:, :, :], ACT.Exp).then_inc(fin_e_ready, 1)

        def dense_start(it, p):
            pass

        def dense(it, p, first, end):
            for g in range(first, end):
                act.wait_ge(pair_mm, GROUPS_D * (2 * it + p) + g + 1)
                A.activation(
                    dense_e[g % 2],
                    p_sim[:, 512 * (g % 2):512 * (g % 2) + 512].rearrange("p (l d t) -> p l d t", d=2, t=T)[:, :, 1, :],
                    ACT.Exp).then_inc(dense_e_ready, 1)

        def back(it, p, following, ahead):
            b = 2 * it + p
            last_batch = isinstance(b, int) and b == B - 1
            if last_batch:
                queries(it, p)
                weigh(it, p, FIRST, EARLY)
            weigh(it, p, EARLY, GATHERED)
            act.wait_ge(kv_mm, GATHERED * b + GATHERED)
            A.copy(kv[:, 3:GATHERED, :].rearrange("t h d -> t (h d)"), p_y[:, 0:512])
            A.copy(kv[:, 0:3, :].rearrange("t h d -> t (h d)"), p_y[:, 512:KV * GATHERED])
            A.activation(kv[:, DENSE, :], p_y[:, at_sum(DENSE)], ACT.Copy,
                         scale=dense_inv[p][:, 0:1]).then_inc(kv_ready, 1)
            act.wait_ge(k_tr, b + 1)
            if last_batch:
                act.wait_ge(out_ready, b)
            for c in range(2):
                last = A.copy(k_t[:, 4 * c:4 * c + 4, :].rearrange("d h t -> d (h t)"),
                              p_x[0:C, 512 * c:512 * c + 512])
            last.then_inc(k_t_ready, 1)
            act.wait_ge(neg_max_ready, b + 1)
            for h in range(HEADS):
                last = A.activation(prob[:, h, :], prob[:, h, :], ACT.Exp, bias=neg_max[:, h:h + 1],
                                    accum_out=row_sum[:, h:h + 1])
            last.then_inc(prob_ready, 1)
            if ahead is not None:
                front_root(*ahead, 1)
            act.wait_ge(prob_tr, b + 1)
            for c in range(2):
                last = A.copy(prob_t[:, 4 * c:4 * c + 4, :].rearrange("j h i -> j (h i)"),
                              p_x[:, 512 * c:512 * c + 512])
            last.then_inc(prob_t_ready, 1)
            if ahead is not None:
                front_root(*ahead, 2)
            if following is not None:
                weigh(*following, 0, 1)
            act.wait_ge(attn_o_tr, b + 1)
            A.copy(attn_o_t[:, :, :].rearrange("d c t -> d (c t)"), p_y[:, 512:1024]).then_inc(attn_o_t_ready, 1)
            if ahead is not None:
                gram_copies(*ahead)
            root(b_var_ready, b_rstd_ready, 4 * b + 1, b_var, b_log, b_rstd0)
            if following is not None:
                dense(*following, 0, 2)
            if ahead is not None:
                attn_m_copy(*ahead)
            act.wait_ge(xh3_tr, b + 1)
            A.copy(xh3_t[:, :], p_back[0:C, 64:192]).then_inc(xh3_t_ready, 1)
            if ahead is not None:
                front_root(*ahead, 3)
            if following is not None:
                dense(*following, 2, 4)
                weigh(*following, 1, 1.5)
            act.wait_ge(neg_kmax_ready, b + 1)
            A.activation(l1_q[:, :], p_back[:, 192:256], ACT.Copy, scale=Q_SCALE)
            A.copy(l1_v_t[:, :], p_back[0:C, 384:512])
            A.activation(ek_t[:, :], p_back[0:C, 256:384], ACT.Exp, bias=neg_kmax[:, 0:1],
                         accum_out=k_sum[:, 0:1]).then_inc(ek_t_ready, 1)
            act.wait_ge(ek_tr, b + 1)
            A.copy(ek[:, :], p_back[:, 64:128]).then_inc(ek_ready, 1)
            if ahead is not None:
                xh2_copy(*ahead)
            if following is not None:
                dense(*following, 4, 6)
                weigh(*following, 1.5, FIRST)
                dense(*following, 6, 8)
            root(b_var_ready, b_rstd_ready, 4 * b + 2, b_var, b_log, b_rstd0)
            if following is not None:
                dense(*following, 8, 12)
            root(b_var_ready, b_rstd_ready, 4 * b + 3, b_var, b_log, b_rstd0)
            if following is not None:
                dense(*following, 12, 14)
            root(b_var_ready, b_rstd_ready, 4 * b + 4, b_var, b_log, b_rstd0)
            if following is not None:
                dense(*following, 14, 16)
            act.wait_ge(xn_tr, b + 1)
            A.copy(xn_t[:, :], p_back[0:C, 64:192]).then_inc(xn_t_ready, 1)
            act.wait_ge(gap_ready, b + 1)
            A.activation(gap_e[:, :], gap[:, :], ACT.Exp).then_inc(gap_e_ready, 1)
            act.wait_ge(hid_mm, b + 1)
            for e in range(E):
                last = A.activation(hid[:, e, :], p_x[:, HID * e:HID * e + HID], ACT.Gelu, bias=b1_sb[:, e:e + 1])
            last.then_inc(hid_ready, 1)
            A.preload_act_table_set("natural_log_exp_and_others")

        over_batches(act, tokens, subkeys, select, dense_start, dense, back)

    @block.tensor
    def _(pe):
        M = nc.tensor.matmul
        TR = nc.tensor.transpose

        pe.wait_ge(consts_loaded, 16 * N_CONST_DMAS)
        pe.wait_ge(pool_consts, POOL_CONSTS)
        for g in range(GROUPS):
            last = M(p_sim[0:C, SUBKEYS * g:SUBKEYS * g + SUBKEYS], wqpk_sb[:, g, :], keys_sb[:, g, :],
                     start=True, stop=True)
        last.then_inc(score_mm, 1)
        pe.wait_ge(score_ready, 1)

        def queries(it, p):
            for h in range(HEADS):
                last = M(p_x[0:C, T * h:T * h + T], wq_sb[:, C * h:C * h + C], xh2_t[p][:, :],
                         start=True, stop=True)
            last.then_inc(q_mm, 1)

        def sum_rows(it, p, first, end):
            b = 2 * it + p
            for h in range(first, end):
                if h == FIRST:
                    hold(pe, sums_free, b + 1)
                hold(pe, scaled, GATHERED * b + h + 1)
                for k in range(TOPK):
                    last = M(p_y[:, at_sum(h)], ident[:, :], gath[p][:, h, k, :],
                             start=(k == 0), stop=(k == TOPK - 1))
                last.then_inc(kv_mm, 1)

        def mean(it, p):
            hold(pe, rowstats_ready, 2 * it + p + 1)
            M(p_front[:, 0:1], mean_w[:, :], rowstat[:, 0:1], start=True, stop=True).then_inc(mean_ready, 1)

        def variance(it, p):
            hold(pe, dev_ready, 2 * it + p + 1)
            M(p_front[:, 1:2], mean_w[:, :], dev_sq[:, :], start=True, stop=True).then_inc(var_ready, 1)

        def gram_product(it, p):
            hold(pe, xh1_ready, 2 * it + p + 1)
            TR(p_front[0:C, 128:256], xh1[:, :], ident[:, :])
            M(p_front[0:C, 256:320], xh1[:, :], xh1[:, :], start=True, stop=True).then_inc(gram_mm, 1)

        def attn_m_product(it, p):
            hold(pe, gram_ready, 2 * it + p + 1)
            M(p_front[0:C, 320:384], attn_w[:, :], gram[:, :], start=True, stop=True).then_inc(attn_m_mm, 1)

        def attn0_product(it, p):
            hold(pe, attn_m_ready, 2 * it + p + 1)
            M(p_front[:, 384:448], xh1_t[:, :], attn_m[:, :], start=True, stop=True).then_inc(attn0_mm, 1)

        def xh2_transpose(it, p):
            hold(pe, xh2_ready, 2 * it + p + 1)
            TR(p_front[0:C, 128:256], xh2[:, :], ident[:, :]).then_inc(xh2_tr, 1)

        def scores(it, p):
            hold(pe, xh2_t_ready, 2 * it + p + 1)
            for c in range(2):
                last = M(p_sim[:, 512 * c:512 * c + 512], xh2_t[p][:, :], score_w[:, 512 * c:512 * c + 512],
                         start=True, stop=True)
            last.then_inc(sim_mm, 1)

        def tokens(it, p):
            for step in (mean, variance, gram_product, attn_m_product, attn0_product, xh2_transpose, scores):
                step(it, p)

        def subkeys(it, p):
            pass

        def select(it, p, before):
            if before is not None:
                queries(*before)
                sum_rows(*before, 0 if isinstance(it, int) else FIRST, EARLY)

        def dense_start(it, p):
            hold(pe, ranks_ready, 2 * it + p + 1)
            TR(p_back[:, 0:128], below.rearrange("t s i -> t (s i)"), ident[:, :])
            for r in range(TOPK):
                last = M(p_back[:, 128:256], rank_hot[:, r, :, :].rearrange("t s i -> t (s i)"), ident_bf[:, :],
                         start=(r == 0), stop=(r == TOPK - 1))
            last.then_inc(ranks_tr, 1)

        def pair_sums(it, p, g):
            if g == 0:
                hold(pe, dense_mov_ready, 2 * it + p + 1)
            if g >= 2:
                hold(pe, dense_w_ready, GROUPS_D * (2 * it + p) + g - 1)
            for l in range(PER_GROUP):
                sel = pair_sel[:, PER_GROUP * g + l, :]
                at = 512 * (g % 2) + 256 * l
                M(p_sim[:, at:at + 256], sel, dense_mov[:, 0:2, :].rearrange("p a t -> p (a t)"),
                  start=True, stop=False, skip_group_check=True)
                M(p_sim[:, at + 128:at + 256], sel, dense_mov[:, 2, :], start=False, stop=False,
                  skip_group_check=True)
                last = M(p_sim[:, at + 128:at + 256], sel, dense_mov[:, 3, :], start=False, stop=True,
                         skip_group_check=True)
            last.then_inc(pair_mm, 1)

        def dense_product(it, p, g):
            hold(pe, dense_w_ready, GROUPS_D * (2 * it + p) + g + 1)
            for l in range(PER_GROUP):
                c = PER_GROUP * g + l
                M(p_y[:, at_sum(DENSE)], dense_w[g % 2][:, l, :], dense_sb[:, c, :],
                  start=(c == 0), stop=(c == CHUNKS - 1))

        def dense(it, p, first, end):
            for g in range(first, end):
                pair_sums(it, p, g)
                if g > first:
                    dense_product(it, p, g - 1)
            dense_product(it, p, end - 1)

        def back(it, p, following, ahead):
            b = 2 * it + p
            last_batch = isinstance(b, int) and b == B - 1
            if last_batch:
                queries(it, p)
            sum_rows(it, p, FIRST if last_batch else EARLY, GATHERED)
            if following is not None:
                dense_start(*following)
            hold(pe, kv_ready, b + 1)
            for h in range(HEADS):
                last = TR(p_x[0:C, T * h:T * h + T], kv[:, h, 0:C], ident[:, :])
            last.then_inc(k_tr, 1)
            if ahead is not None:
                mean(*ahead)
                variance(*ahead)
            hold(pe, q_ready, b + 1)
            hold(pe, k_t_ready, b + 1)
            for h in range(HEADS):
                last = M(p_y[:, T * h:T * h + T], q_t[:, h, :], k_t[:, h, :], start=True, stop=True)
            last.then_inc(s_mm, 1)
            hold(pe, prob_ready, b + 1)
            for h in range(HEADS):
                last = TR(p_x[:, T * h:T * h + T], prob[:, h, :], ident[:, :])
            last.then_inc(prob_tr, 1)
            hold(pe, prob_t_ready, b + 1)
            for h in range(HEADS):
                last = M(p_y[:, C * h:C * h + C], prob_t[:, h, :], kv[:, h, C:KV], start=True, stop=True)
            last.then_inc(attn_mm, 1)
            hold(pe, attn_o_ready, b + 1)
            for c in range(HEADS * C // 128):
                last = TR(p_y[:, 512 + T * c:512 + T * c + T], attn_o[:, 128 * c:128 * c + 128], ident[:, :])
            last.then_inc(attn_o_tr, 1)
            if ahead is not None:
                gram_product(*ahead)
            hold(pe, attn_o_t_ready, b + 1)
            n = HEADS * C // 128
            for c in range(n):
                last = M(p_back[:, 0:C], attn_o_t[:, c, :], wo_sb[:, c, :], start=(c == 0), stop=(c == n - 1))
            last.then_inc(wo_mm, 1)
            if following is not None:
                dense(*following, 0, 2)
            if ahead is not None:
                attn_m_product(*ahead)
            hold(pe, xh3_ready, b + 1)
            TR(p_back[0:C, 64:192], xh3[:, :], ident[:, :]).then_inc(xh3_tr, 1)
            if ahead is not None:
                attn0_product(*ahead)
            hold(pe, xh3_t_ready, b + 1)
            M(p_back[:, 192:256], xh3_t[:, :], wqkv_sb[:, 0:C], start=True, stop=True)
            M(p_back[0:C, 256:384], wqkv_sb[:, C:2 * C], xh3_t[:, :], start=True, stop=True)
            M(p_back[0:C, 384:512], wqkv_sb[:, 2 * C:3 * C], xh3_t[:, :], start=True, stop=True
              ).then_inc(qkv_mm, 1)
            if following is not None:
                dense(*following, 2, 4)
            hold(pe, ek_t_ready, b + 1)
            TR(p_back[:, 64:128], ek_t[:, :], ident[0:C, 0:C]).then_inc(ek_tr, 1)
            if ahead is not None:
                xh2_transpose(*ahead)
            if following is not None:
                dense(*following, 4, 6)
            hold(pe, ek_ready, b + 1)
            M(p_back[0:C, 128:192], ek[:, :], l1_q[:, :], start=True, stop=True).then_inc(l1_a_mm, 1)
            hold(pe, l1_a_ready, b + 1)
            M(p_back[0:C, 256:384], l1_a[:, :], l1_v_t[:, :], start=True, stop=True).then_inc(l1_o_mm, 1)
            if following is not None:
                dense(*following, 6, 8)
            hold(pe, l1_x_ready, b + 1)
            for j in range(L1_HEADS):
                last = M(p_back[:, 0:C], l1_x[:, j, :, :].rearrange("d h m -> d (h m)"), wout_sb[:, j, :],
                         start=(j == 0), stop=(j == L1_HEADS - 1))
            last.then_inc(l1_mm, 1)
            if following is not None:
                dense(*following, 8, 16)
            hold(pe, xn_ready, b + 1)
            TR(p_back[0:C, 64:192], xn[:, :], ident[:, :]).then_inc(xn_tr, 1)
            hold(pe, xn_t_ready, b + 1)
            M(p_back[:, 192:192 + E], xn_t[:, :], wr_sb[:, :], start=True, stop=True).then_inc(logit_mm, 1)
            if ahead is not None:
                scores(*ahead)
            for e in range(E):
                last = M(p_x[:, HID * e:HID * e + HID], w1_sb[:, e, :], xn_t[:, :], start=True, stop=True)
            last.then_inc(hid_mm, 1)
            if following is not None:
                sum_rows(*following, 0, 1)
            hold(pe, hid_ready, b + 1)
            for e in range(E):
                last = M(p_y[:, C * e:C * e + C], hid[:, e, :], w2_sb[:, e, :], start=True, stop=True)
            last.then_inc(y_mm, 1)
            if following is not None:
                sum_rows(*following, 1, FIRST)

        over_batches(pe, tokens, subkeys, select, dense_start, dense, back)

    ctx.close()


def kernel(**inputs):
    import numpy as np
    import concourse.bacc as bacc
    from concourse.bass_utils import run_bass_kernel_spmd

    g = {k: np.asarray(v) for k, v in inputs.items()}
    spread = {"conv_w": g["L0_tok_w"], "conv_b": g["L0_tok_b"], "tok_gamma": g["L0_tok_gamma"],
              "tok_beta": g["L0_tok_beta"], "tok_alpha": g["L0_tok_alpha"], "bout": g["L1_attn_bout"],
              "l1_gamma": g["L1_attn_gamma"], "l1_beta": g["L1_attn_beta"], "ffn_gamma": g["L1_ffn_gamma"],
              "ffn_beta": g["L1_ffn_beta"], "br": g["L1_ffn_br"], "b2": g["L1_ffn_b2"]}
    rows = np.concatenate([spread[n].reshape(-1) for n in ROWS])
    arrays = {
        "x": g["x"],
        "rows": np.broadcast_to(rows[None, :], (T, ROW_WORDS)),
        "attn_w": g["L0_attn_W"],
        "wqpk_t": g["L0_ffn_Wq_pk"].reshape(C, GROUPS, DKEY).transpose(2, 1, 0),
        "keys_t": g["L0_ffn_pk_keys"].transpose(3, 0, 2, 1).reshape(DKEY, GROUPS, SUBKEYS),
        "wq": g["L0_ffn_Wq"],
        "table": np.concatenate([g["L0_ffn_keys_table"], g["L0_ffn_values_table"]], axis=1),
        "wo": g["L0_ffn_Wo"].reshape(-1, 128, C).transpose(1, 0, 2),
        "wqkv": g["L1_attn_Wqkv"],
        "wout": np.tile(g["L1_attn_Wout"].reshape(-1, C // L1_HEADS, C).transpose(1, 0, 2), (L1_HEADS, 1, 1)),
        "wr": g["L1_ffn_Wr"],
        "w1": g["L1_ffn_W1"].transpose(1, 0, 2),
        "b1_t": g["L1_ffn_b1"].transpose(1, 0),
        "w2": g["L1_ffn_W2"].transpose(1, 0, 2),
    }
    last_head = slice(DENSE * SUBKEYS * SUBKEYS, HEADS * SUBKEYS * SUBKEYS)
    arrays["dense_t"] = arrays["table"][last_head].reshape(CHUNKS, 128, KV).transpose(1, 0, 2)
    arrays = {k: np.ascontiguousarray(v) for k, v in arrays.items()}
    nc = bacc.Bacc("TRN2", target_bir_lowering=False, num_devices=1)
    args = [nc.dram_tensor(f"in_{k}", v.shape, F32, kind="ExternalInput").ap() for k, v in arrays.items()]
    out = nc.dram_tensor("out", (B, T, C), F32, kind="ExternalOutput").ap()
    build(nc, *args, out)
    r = run_bass_kernel_spmd(nc, [{f"in_{k}": v for k, v in arrays.items()}], core_ids=[0])
    return r.results[0]["out"]
```
